# Optimizing a Trainium2 kernel written in Bass

```python
import numpy as np
import jax
import jax.numpy as jnp

def _softmax(x, axis=-1):
    return jax.nn.softmax(x, axis=axis)

def _gelu(x):
    return jax.nn.gelu(x, approximate=True)

def _silu(x):
    return jax.nn.silu(x)

def _sigmoid(x):
    return jax.nn.sigmoid(x)

def _layernorm(x, axis=-1, eps=1e-05):
    m = jnp.mean(x, axis=axis, keepdims=True)
    v = jnp.var(x, axis=axis, keepdims=True)
    return (x - m) / jnp.sqrt(v + eps)

def _scatter_add(tgt, idx, src, axis=0):
    return tgt.at[idx].add(src)

def _segment_sum(src, seg, n):
    return jax.ops.segment_sum(src, seg, n)
kernel_name = 'mk_gnn_resnorm_d2_gnn_r64_2556ac'

def setup_inputs(seed: int=0):
    np.random.seed(seed)
    _w = jnp.asarray

    def _rec_inputs():
        import jax
        import jax.numpy as jnp
        _gk = jax.random.key(seed)
        x = -0.0003713 + 1 * jax.random.normal(jax.random.fold_in(_gk, 1), (50000, 256), jnp.float32)
        src = jax.random.randint(jax.random.fold_in(_gk, 2), (25000,), 0, 50000, jnp.int32)
        dst = jax.random.randint(jax.random.fold_in(_gk, 3), (25000,), 0, 50000, jnp.int32)
        _o = jnp.argsort(dst, stable=True)
        src = src[_o]
        dst = dst[_o]
        edge_type_16 = jax.random.randint(jax.random.fold_in(_gk, 13), (25000,), 0, 16, jnp.int32)
        edge_weight = jax.random.uniform(jax.random.fold_in(_gk, 14), (25000,), jnp.float32, 0.0, 0.03125)
        return (x, src, dst, edge_type_16, edge_weight)
    x, src, dst, edge_type_16, edge_weight = _rec_inputs()

    def _L0_gnn_setup():
        import jax, jax.numpy as jnp
        import numpy as np
        NUM_BLOCKS = 64

        def rgcn_layer(x, src, dst, edge_type, W, root, bias):
            N, d = x.shape
            xj = x[src]
            out0 = x @ root + bias

            def body(out, inputs):
                r, Wr = inputs
                mask = (edge_type == r).astype(x.dtype)
                s = jax.ops.segment_sum(xj * mask[:, None], dst, num_segments=N)
                cnt = jax.ops.segment_sum(mask, dst, num_segments=N)
                h = s / jnp.maximum(cnt, 1.0)[:, None]
                hb = h.reshape(N, NUM_BLOCKS, d // NUM_BLOCKS)
                out = out + jnp.einsum('nbi,bio->nbo', hb, Wr).reshape(N, d)
                return (out, None)
            R = W.shape[0]
            out, _ = jax.lax.scan(body, out0, (jnp.arange(R), W))
            return out
        key = jax.random.key(seed)
        ks = jax.random.split(key, 9)
        N, d, R, E = (50000, 256, 16, 12500)
        db = d // NUM_BLOCKS
        return {'node_emb': jax.random.normal(ks[0], (N, d), jnp.float32), 'edge_index': jax.random.randint(ks[1], (2, E), 0, N), 'edge_type': jax.random.randint(ks[2], (E,), 0, R), 'W1': jax.random.normal(ks[3], (R, NUM_BLOCKS, db, db), jnp.float32) * 0.1, 'root1': jax.random.normal(ks[4], (d, d), jnp.float32) * 0.05, 'bias1': jnp.zeros((d,), jnp.float32), 'W2': jax.random.normal(ks[5], (R, NUM_BLOCKS, db, db), jnp.float32) * 0.1, 'root2': jax.random.normal(ks[6], (d, d), jnp.float32) * 0.05, 'bias2': jnp.zeros((d,), jnp.float32)}
    _L0_gnn_all = _L0_gnn_setup()
    _L0_gnn_in = {k: v for k, v in _L0_gnn_all.items() if k in ('W1', 'root1', 'bias1', 'W2', 'root2', 'bias2')}
    del _L0_gnn_all

    def _L1_gnn_setup():
        import jax, jax.numpy as jnp
        import numpy as np
        N_NODES = 100000
        N_EDGES = 50000
        DIM = 256
        LEAKY_SLOPE = 0.2
        EPS = 1e-12
        key = jax.random.key(seed)
        ks = jax.random.split(key, 8)
        embeddings = jax.random.normal(ks[0], (N_NODES, DIM), dtype=jnp.float32)
        edge_src = jax.random.randint(ks[1], (N_EDGES,), 0, N_NODES, dtype=jnp.int32)
        edge_dst = jax.random.randint(ks[2], (N_EDGES,), 0, N_NODES, dtype=jnp.int32)
        edge_val = jax.random.uniform(ks[3], (N_EDGES,), dtype=jnp.float32) / 32.0
        scale = 1.0 / np.sqrt(DIM)
        W1 = jax.random.normal(ks[4], (DIM, DIM), dtype=jnp.float32) * scale
        b1 = jax.random.normal(ks[5], (DIM,), dtype=jnp.float32) * 0.01
        W2 = jax.random.normal(ks[6], (DIM, DIM), dtype=jnp.float32) * scale
        b2 = jax.random.normal(ks[7], (DIM,), dtype=jnp.float32) * 0.01
        return {'embeddings': embeddings, 'edge_src': edge_src, 'edge_dst': edge_dst, 'edge_val': edge_val, 'W1': W1, 'b1': b1, 'W2': W2, 'b2': b2}
    _L1_gnn_all = _L1_gnn_setup()
    _L1_gnn_in = {k: v for k, v in _L1_gnn_all.items() if k in ('W1', 'b1', 'W2', 'b2')}
    del _L1_gnn_all
    return {'x': x, 'src': src, 'dst': dst, 'edge_type_16': edge_type_16, 'edge_weight': edge_weight, 'L0_gnn_W1': _L0_gnn_in['W1'], 'L0_gnn_root1': _L0_gnn_in['root1'], 'L0_gnn_bias1': _L0_gnn_in['bias1'], 'L0_gnn_W2': _L0_gnn_in['W2'], 'L0_gnn_root2': _L0_gnn_in['root2'], 'L0_gnn_bias2': _L0_gnn_in['bias2'], 'L1_gnn_W1': _L1_gnn_in['W1'], 'L1_gnn_b1': _L1_gnn_in['b1'], 'L1_gnn_W2': _L1_gnn_in['W2'], 'L1_gnn_b2': _L1_gnn_in['b2']}

def reference(x, src, dst, edge_type_16, edge_weight, L0_gnn_W1, L0_gnn_root1, L0_gnn_bias1, L0_gnn_W2, L0_gnn_root2, L0_gnn_bias2, L1_gnn_W1, L1_gnn_b1, L1_gnn_W2, L1_gnn_b2):
    import jax
    import jax.numpy as jnp

    def _L0_gnn_ref(node_emb, edge_index, edge_type, W1, root1, bias1, W2, root2, bias2):
        import jax, jax.numpy as jnp
        import numpy as np
        NUM_BLOCKS = 64

        def rgcn_layer(x, src, dst, edge_type, W, root, bias):
            N, d = x.shape
            xj = x[src]
            out0 = x @ root + bias

            def body(out, inputs):
                r, Wr = inputs
                mask = (edge_type == r).astype(x.dtype)
                s = jax.ops.segment_sum(xj * mask[:, None], dst, num_segments=N)
                cnt = jax.ops.segment_sum(mask, dst, num_segments=N)
                h = s / jnp.maximum(cnt, 1.0)[:, None]
                hb = h.reshape(N, NUM_BLOCKS, d // NUM_BLOCKS)
                out = out + jnp.einsum('nbi,bio->nbo', hb, Wr).reshape(N, d)
                return (out, None)
            R = W.shape[0]
            out, _ = jax.lax.scan(body, out0, (jnp.arange(R), W))
            return out
        src, dst = (edge_index[0], edge_index[1])
        x = jax.nn.relu(rgcn_layer(node_emb, src, dst, edge_type, W1, root1, bias1))
        x = rgcn_layer(x, src, dst, edge_type, W2, root2, bias2)
        return x

    def _L1_gnn_ref(embeddings, edge_src, edge_dst, edge_val, W1, b1, W2, b2):
        import jax, jax.numpy as jnp
        import numpy as np
        N_NODES = 100000
        N_EDGES = 50000
        DIM = 256
        LEAKY_SLOPE = 0.2
        EPS = 1e-12
        ego_emb = embeddings @ W1.T + b1
        messages = edge_val[:, None] * embeddings[edge_src]
        neighbor_emb = jax.ops.segment_sum(messages, edge_dst, num_segments=embeddings.shape[0])
        interaction_emb = neighbor_emb * embeddings
        side_emb = (neighbor_emb + interaction_emb) @ W2.T + b2
        out = ego_emb + side_emb
        out = jnp.where(out >= 0, out, LEAKY_SLOPE * out)
        norm = jnp.sqrt(jnp.sum(out * out, axis=1, keepdims=True))
        return out / jnp.maximum(norm, EPS)
    edge_index = jnp.stack([src, dst])
    x = _layernorm(x + _L0_gnn_ref(x, edge_index, edge_type_16, L0_gnn_W1, L0_gnn_root1, L0_gnn_bias1, L0_gnn_W2, L0_gnn_root2, L0_gnn_bias2), axis=-1)
    x = _layernorm(x + _L1_gnn_ref(x, src, dst, edge_weight, L1_gnn_W1, L1_gnn_b1, L1_gnn_W2, L1_gnn_b2), axis=-1)
    return x

_drawn_inputs = setup_inputs


def setup_inputs(seed=0):
    import zlib

    import numpy as np

    out = dict(_drawn_inputs(seed))
    spreads = {'L0_gnn_bias1': (0.0, 0.1), 'L0_gnn_bias2': (0.0, 0.1)}
    factors = {'edge_weight': 36.631, 'L1_gnn_b1': 64.0, 'L1_gnn_W2': 8.0, 'L1_gnn_b2': 64.0}
    for name, (base, spread) in spreads.items():
        noise = np.random.default_rng([zlib.crc32(name.encode()), seed]).standard_normal(out[name].shape)
        drawn = base * np.exp(spread * noise) if base else spread * noise
        out[name] = jnp.asarray(drawn.astype(out[name].dtype))
    for name, factor in factors.items():
        out[name] = (out[name] * factor).astype(out[name].dtype)
    return out
```

```python
from contextlib import ExitStack

import concourse.bass as bass
from concourse import mybir

P = 128
U = 12
HALF = 3
SLOTS = U // HALF
RUN = 8
FIELDS = 8
SOURCE, TARGET, RELATION, SHARE, WEIGHT = range(5)
SHIFTS = 2 * RUN + 1
BIG = float(1 << 21)
EPS = 1e-5
SLOPE = 0.2
MIN_NORM = 1e-12

F32 = mybir.dt.float32
BF16 = mybir.dt.bfloat16
I32 = mybir.dt.int32
ALU = mybir.AluOpType
ACT = mybir.ActivationFunctionType
AX_X = mybir.AxisListType.X


def constants(N, REL):
    import numpy as np

    T = -(-N // P)
    cols = np.arange(P)
    part_rows = np.where((cols < 96) & (cols % 32 <= REL), cols % 32, -1)
    bounds = [P * t for t in range(T)] + [N - P, N]
    rows = [np.tile(np.asarray(a, np.float32), (P, 1)) for a in (cols, part_rows, bounds)]
    earlier = np.tril(np.ones((P, P), np.float32), -1)
    return np.ascontiguousarray(np.concatenate([np.eye(P, dtype=np.float32), *rows, earlier], 1))


def own_edges(N, REL):
    import numpy as np

    own = np.zeros((N, FIELDS), np.float32)
    own[:, SOURCE] = own[:, TARGET] = np.arange(N)
    own[:, RELATION], own[:, SHARE], own[:, WEIGHT] = REL, 1, 1
    return own


def run_ahead(eng, ops, T):
    most = max(lead for _, lead in ops)
    loops = (T - HALF - most) // U
    for t in range(-most, 0):
        for op, lead in ops:
            if t + lead >= 0:
                op(t + lead, (t + lead) % U, (t + lead) // U)
    with eng.Fori(0, loops) as g:
        for k in range(U):
            for op, lead in ops:
                op(g * U + (k + lead), (k + lead) % U, g + (k + lead) // U)
    for t in range(loops * U, T):
        for op, lead in ops:
            if t + lead < T:
                op(t + lead, (t + lead) % U, (t + lead) // U)


def build(nc, x, src, dst, kind, weight, split_whole, root1, root2, w1t, w2t, consts, own_rows, out, REL, BI):
    N, D = x.shape
    E = src.shape[0]
    W4 = BI * D
    K = D // P
    T = -(-N // P)
    LAST = T - 1
    OVERLAP = P * T - N
    EP = max(k for k in range(1, P + 1) if E % k == 0)
    EJ = E // EP
    EROWS = E + P
    NB = T + 2
    NHALF = -(-T // HALF)
    CHUNKS = -(-E // P)
    ZERO_ROWS = 2 * W4 // D * P
    STEPS = -(-(2 * E + 1) // SHIFTS)
    KEYS_AT = E + SHIFTS
    assert LAST % HALF == 0 and N >= P and K == 2 and W4 == 1024 and NB <= 512 and REL < 32

    ctx = ExitStack()
    with ctx:
        def sb(name, shape, dt=F32):
            return ctx.enter_context(nc.sbuf_tensor(name, shape, dt))

        def ps(name, shape, dt=F32):
            return ctx.enter_context(nc.psum_tensor(name, shape, dt))

        def sem(name):
            return ctx.enter_context(nc.semaphore(name))

        hidden = nc.dram_tensor("hidden", [N, D], F32).ap()
        mid = nc.dram_tensor("mid", [N, D], F32).ap()
        edge_rows = nc.dram_tensor("edge_rows", [EROWS + N, FIELDS], F32).ap()
        dst_flat = nc.dram_tensor("dst_flat", [1, EROWS], F32).ap()
        key_flat = nc.dram_tensor("key_flat", [1, E + 2 * KEYS_AT], F32).ap()
        sums = nc.dram_tensor("sums", [N, D], F32).ap()

        const = sb("const", [P, consts.shape[1]])
        eye = const[:, 0:P]
        iota = const[:, P:2 * P]
        rel_iota = const[:, 2 * P:3 * P]
        bounds = const[:, 3 * P:3 * P + NB]
        earlier = const[:, 3 * P + NB:4 * P + NB]
        eye16 = sb("eye16", [P, P], BF16)
        ones16 = sb("ones16", [P, P], BF16)
        ones32 = sb("ones32", [P, 1])
        root1_sb = sb("root1_sb", [P, K, D])
        root2_sb = sb("root2_sb", [P, K, D])
        w1_sb = sb("w1_sb", [P, K, D])
        w2_sb = sb("w2_sb", [P, K, D])
        parts = sb("parts", [P, 2 * W4 + 3 * D], BF16)
        edges = sb("edges", [P, T, FIELDS])
        local = sb("local", [P, T])
        far = sb("far", [P, HALF])
        node_of = sb("node_of", [P, T], I32)
        xt = sb("xt", [P, U, D])
        ht = sb("ht", [P, U, D])
        res = sb("res", [P, U, D])
        y = sb("y", [P, U, D])
        gath = sb("gath", [P, U, D])
        gidx = sb("gidx", [P, U], I32)
        xT = sb("xT", [P, 2, D])
        mT = sb("mT", [P, 2, D])
        rel_hot = sb("rel_hot", [P, 2, P], BF16)
        rel_hotT = sb("rel_hotT", [P, 2, P], BF16)
        prod = sb("prod", [P, 2, W4])
        pair = sb("pair", [P, 2, W4 // 2])
        msg = sb("msg", [P, 2, D])
        node_hot = sb("node_hot", [P, 2, P])
        junk = sb("junk", [P, 4, D])
        slant = sb("slant", [P, 2, D])
        st_sum = sb("st_sum", [P, U])
        st_neg = sb("st_neg", [P, U])
        st_sq = sb("st_sq", [P, U])
        st_root = sb("st_root", [P, U])
        st_ysq = sb("st_ysq", [P, U])
        eps = sb("eps", [P, 1])
        st_rstd = sb("st_rstd", [P, U])
        st_shift = sb("st_shift", [P, U])
        st_norm = sb("st_norm", [P, U])
        st_clip = sb("st_clip", [P, U])
        st_scale = sb("st_scale", [P, U])
        words = sb("words", [EP, 3, EJ], I32)
        weight_in = sb("weight_in", [EP, EJ])
        rows = sb("rows", [EP, EJ, FIELDS])
        keys = sb("keys", [EP, EJ])
        no_keys = sb("no_keys", [EP, EJ])
        dstf = sb("dstf", [EP, EJ])
        halo = sb("halo", [EP, EJ + 2 * RUN])
        equal = sb("equal", [EP, SHIFTS, EJ])
        dst_halo = sb("dst_halo", [EP, EJ + RUN])
        unsorted = sb("unsorted", [EP, 2, EJ])
        trouble = sb("trouble", [EP, 1])
        row = sb("row", [1, 3, NB])
        general = sb("general", [1, 4])
        general_i = sb("general_i", [1, 1], I32)
        count = sb("count", [EP, EJ])
        more = sb("more", [EP, EJ])
        below = sb("below", [EP, 2, NB])
        start_i = sb("start_i", [1, NB], I32)
        pad_key = sb("pad_key", [1, RUN])
        pad_dst = sb("pad_dst", [1, P])
        pad_rows = sb("pad_rows", [P, FIELDS])
        whole = sb("whole", [P, 2 * W4 + 3 * D])
        rest = sb("rest", [P, 2 * W4 + 3 * D])

        ch_rows = sb("ch_rows", [P, FIELDS])
        ch_dst = sb("ch_dst", [P, P])
        ch_same = sb("ch_same", [P, P])
        ch_before = sb("ch_before", [P, P])
        ch_idx = sb("ch_idx", [P, 1], I32)
        ch_to = sb("ch_to", [P, 1], I32)
        ch_dup = sb("ch_dup", [P, 2])
        ch_old = sb("ch_old", [P, D])
        ch_sum = sb("ch_sum", [P, D])

        ps_w = ps("ps_w", [P, 2, W4])
        ps_o = ps("ps_o", [P, 2, 512])
        ps_x = ps("ps_x", [P, 1, D])
        ps_r = ps("ps_r", [P, 1, P], BF16)
        ps_n = ps_w[:, 0, :].rearrange("p (s d) -> p s d", s=2)[:, :, 0:D]
        ps_m = ps_w[:, 1, :].rearrange("p (s d) -> p s d", s=2)[:, :, 0:D]

        loaded = sem("loaded")
        dve_done = sem("dve_done")
        below_done = sem("below_done")
        starts_counted = sem("starts_counted")
        starts_ready = sem("starts_ready")
        keys_out = sem("keys_out")
        keys_in_dram = sem("keys_in_dram")
        halo_in = sem("halo_in")
        rows_out = sem("rows_out")
        rows_in_dram = sem("rows_in_dram")
        window_in = [sem(f"window_in{k}") for k in range(U)]
        window_local = sem("window_local")
        window_far = sem("window_far")
        window_ready = sem("window_ready")
        setup_done = sem("setup_done")
        dst_in_dram = sem("dst_in_dram")
        dst_halo_in = sem("dst_halo_in")
        trouble_found = sem("trouble_found")
        trouble_summed = sem("trouble_summed")
        path_known = sem("path_known")
        no_keys_out = sem("no_keys_out")
        shifts_in = sem("shifts_in")
        shift_equal, shift_more = sem("shift_equal"), sem("shift_more")
        shifts_counted = sem("shifts_counted")
        sums_zero, zero_tile = sem("sums_zero"), sem("zero_tile")
        ch_in = sem("ch_in")
        ch_idx_ready = sem("ch_idx_ready")
        ch_gathered = sem("ch_gathered")
        ch_hot, ch_hot_ps, ch_hotT, ch_w_ps = sem("ch_hot"), sem("ch_hot_ps"), sem("ch_hotT"), sem("ch_w_ps")
        ch_prod, ch_pair, ch_raw, ch_msg = sem("ch_prod"), sem("ch_pair"), sem("ch_raw"), sem("ch_msg")
        ch_equal, ch_pairs, ch_count, ch_dups = sem("ch_equal"), sem("ch_pairs"), sem("ch_count"), sem("ch_dups")
        ch_to_ready = sem("ch_to_ready")
        ch_sum_ps = sem("ch_sum_ps")
        ch_before_in = sem("ch_before_in")
        ch_ready = sem("ch_ready")
        ch_stored = sem("ch_stored")
        split_in = sem("split_in")

        gathered = [sem(f"gathered{k}") for k in range(U)]

        class Signals:

            def __init__(self, n):
                def own(name):
                    return sem(f"p{n}_{name}")

                self.x_in = [own(f"x_in{q}") for q in range(SLOTS)]
                self.stored = [own(f"stored{q}") for q in range(SLOTS)]
                self.gathered, self.gathered_before = gathered, [16 * (n - 1) * len(range(k, T, U)) for k in range(U)]
                self.idx = own("idx")
                self.xT_ps, self.xT = own("xT_ps"), own("xT")
                self.node_hot, self.msg = own("node_hot"), own("msg")
                self.o_ps, self.final = own("o_ps"), own("final")
                if n < 3:
                    self.hot, self.hot_ps, self.hotT = own("hot"), own("hot_ps"), own("hotT")
                    self.w_ps, self.prod, self.pair = own("w_ps"), own("prod"), own("pair")
                if n == 2:
                    self.h_in = [own(f"h_in{q}") for q in range(SLOTS)]
                if n > 1:
                    self.sum, self.neg, self.sq = own("sum"), own("neg"), own("sq")
                    self.root, self.rstd, self.shift = own("root"), own("rstd"), own("shift")
                if n == 3:
                    self.n_ps, self.mT_ps, self.mT = own("n_ps"), own("mT_ps"), own("mT")
                    self.slant, self.y, self.ysq = own("slant"), own("y"), own("ysq")
                    self.clip, self.norm, self.scale = own("clip"), own("norm"), own("scale")

        passes = [Signals(1), Signals(2), Signals(3)]

        def pass_stored(eng, s):
            for q in range(SLOTS):
                uses = len(range(q, NHALF, SLOTS))
                eng.wait_ge(s.stored[q], 16 * (uses + 1))

        def prime(eng, *sems):
            for a in sems:
                eng.sem_inc(a, U)

        def at(u, n=1):
            return slice(u, u + n) if isinstance(u, int) else bass.ds(u, n)

        def half_count(u, k, g):
            return (u // HALF if isinstance(u, int) else g * SLOTS + k // HALF) + 1

        def half_slots(u, k):
            if isinstance(u, int) and u == LAST:
                return slice(k, k + 1)
            return slice(k - HALF + 1, k + 1) if k % HALF == HALF - 1 else None

        def tile_rows(u, n):
            if isinstance(u, int) and u == LAST:
                return slice(N - P, N)
            return slice(u * P, (u + n) * P) if isinstance(u, int) else bass.ds(u * P, n * P)

        block = ctx.enter_context(nc.Block())

        @block.sync
        def _(sp):
            for to, of in ((const[:], consts), (words[:, 0, :], src.rearrange("(p j) -> p j", p=EP)),
                           (words[:, 1, :], dst.rearrange("(p j) -> p j", p=EP)),
                           (words[:, 2, :], kind.rearrange("(p j) -> p j", p=EP)),
                           (weight_in[:], weight.rearrange("(p j) -> p j", p=EP)),
                           (root1_sb[:], root1.rearrange("(k p) n -> p k n", k=K)),
                           (root2_sb[:], root2.rearrange("(k p) n -> p k n", k=K)),
                           (w1_sb[:], w1t.rearrange("(k p) n -> p k n", k=K)),
                           (w2_sb[:], w2t.rearrange("(k p) n -> p k n", k=K))):
                sp.dma_start(to, of).then_inc(loaded, 16)
            for r in (0, 32, 64):
                sp.dma_start(whole[r:r + 32, :], split_whole).then_inc(split_in, 16)
            sp.wait_ge(keys_out, 2)
            sp.dma_start(dst_flat[0, 0:E].rearrange("(p j) -> p j", p=EP), dstf[:]).then_inc(dst_in_dram, 16)
            sp.dma_start(dst_flat[:, E:EROWS], pad_dst[:]).then_inc(dst_in_dram, 16)
            sp.dma_start(key_flat[0, KEYS_AT:KEYS_AT + E].rearrange("(p j) -> p j", p=EP), keys[:]).then_inc(keys_in_dram, 16)
            sp.dma_start(key_flat[:, KEYS_AT - RUN:KEYS_AT], pad_key[:]).then_inc(keys_in_dram, 16)
            sp.dma_start(key_flat[:, KEYS_AT + E:KEYS_AT + E + RUN], pad_key[:]).then_inc(keys_in_dram, 16)
            sp.dma_start(edge_rows[E:E + P, :], pad_rows[:]).then_inc(rows_in_dram, 16)
            sp.wait_ge(keys_in_dram, 48)
            wide = bass.AP(key_flat.tensor, KEYS_AT - RUN, [[EJ, EP], [1, EJ + 2 * RUN]])
            sp.dma_start(halo[:], wide).then_inc(halo_in, 16)
            sp.wait_ge(dst_in_dram, 32)
            wide = bass.AP(dst_flat.tensor, 0, [[EJ, EP], [1, EJ + RUN]])
            sp.dma_start(dst_halo[:], wide).then_inc(dst_halo_in, 16)
            sp.wait_ge(path_known, 1)
            slow = sp.value_load(general_i[0:1, 0:1], min_val=0, max_val=1)
            with sp.If(slow):
                sp.dma_start(edge_rows[EROWS:EROWS + N, :], own_rows).then_inc(no_keys_out, 16)
                for first in (SHIFTS - RUN, KEYS_AT + E + RUN):
                    sp.dma_start(key_flat[0, first:first + E].rearrange("(p j) -> p j", p=EP),
                                 no_keys[:]).then_inc(no_keys_out, 16)
                sp.dma_start(key_flat[:, KEYS_AT + 2 * E + RUN:KEYS_AT + 2 * (E + RUN)], pad_key[:]).then_inc(no_keys_out, 16)
                sp.wait_ge(no_keys_out, 64)
                with sp.Fori(0, STEPS) as i:
                    sp.wait_ge(shifts_counted, i + 1)
                    wide = bass.AP(key_flat.tensor, i * SHIFTS + (KEYS_AT - E), [[EJ, EP], [1, EJ + 2 * RUN]])
                    sp.dma_start(halo[:], wide).then_inc(shifts_in, 16)
            sp.wait_ge(rows_out, 1)
            sp.dma_start(edge_rows[0:E, :].rearrange("(p j) f -> p (j f)", p=EP),
                         rows[:].rearrange("p j f -> p (j f)")).then_inc(rows_in_dram, 16)
            sp.wait_ge(starts_ready, 1)
            sp.wait_ge(rows_in_dram, 32)

            def window(u, k, g):
                col = T if isinstance(u, int) and u == LAST else u
                sp.wait_ge(window_ready, half_count(u, k, g))
                start = sp.value_load(start_i[0:1, at(col)], min_val=0, max_val=EROWS + N - P)
                sp.dma_start(edges[:, at(u), :].rearrange("p t f -> p (t f)"),
                             edge_rows[bass.ds(start, P), :]).then_inc(window_in[k], 16)

            def load(s, ring, arrived, of, freed):
                def op(u, k, g):
                    if k % HALF:
                        return
                    m = 1 if isinstance(u, int) and u == LAST else HALF
                    sp.wait_ge(freed, u + (HALF - 1) - U + 1 + U)
                    sp.dma_start(ring[:, k:k + m, :],
                                 of[tile_rows(u, m), :].rearrange("(t p) d -> p t d", p=P)).then_inc(arrived[k // HALF], 16)
                return op

            def store(s, ring, to):
                def op(u, k, g):
                    if isinstance(u, int) and u == LAST:
                        sp.wait_ge(s.final, u + 1 + U)
                        sp.dma_start(to[N - P + OVERLAP:N, :], ring[OVERLAP:P, k, :]).then_inc(s.stored[k // HALF], 16)
                    elif k % HALF == HALF - 1:
                        sp.wait_ge(s.final, u + 1 + U)
                        sp.dma_start(to[tile_rows(u - (HALF - 1), HALF), :].rearrange("(t p) d -> p t d", p=P),
                                     ring[:, k - (HALF - 1):k + 1, :]).then_inc(s.stored[k // HALF], 16)
                return op

            s = passes[0]
            for q in range(SLOTS):
                sp.sem_inc(s.stored[q], 16)
            run_ahead(sp, [(window, 15), (load(s, xt, s.x_in, x, s.xT_ps), 12), (store(s, y, hidden), 0)], T)
            pass_stored(sp, s)
            s = passes[1]
            for q in range(SLOTS):
                sp.sem_inc(s.stored[q], 16)
            run_ahead(sp, [(load(s, ht, s.h_in, hidden, s.xT_ps), 12), (load(s, xt, s.x_in, x, s.sum), 12),
                           (store(s, y, mid), 0)], T)
            pass_stored(sp, s)
            s = passes[2]
            for q in range(SLOTS):
                sp.sem_inc(s.stored[q], 16)
            run_ahead(sp, [(load(s, xt, s.x_in, mid, s.sum), 15), (store(s, ht, out), 0)], T)
            pass_stored(sp, s)

        def slot_stored(eng, s, k, g):
            eng.wait_ge(s.stored[k // HALF], (g + 1) * 16)

        def gathers(pool, s, table, used, last_row):
            def take_idx(u, k, g):
                m = HALF
                if isinstance(u, int) and u == LAST:
                    m = 1
                elif k % HALF != HALF - 1:
                    return
                lo, first = k - m + 1, u - m + 1
                pool.wait_ge(window_ready, half_count(u, k, g) + SLOTS)
                pool.wait_ge(used, u - U + 1 + U)
                nc.gpsimd.tensor_copy(gidx[:, lo:k + 1], node_of[:, at(first, m)]).then_inc(s.idx, 1)

            def gather(u, k, g):
                pool.wait_ge(s.idx, half_count(u, k, g))
                pool.wait_ge(used, u - U + 1 + U)
                pool.nop(nofuse=True)
                nc.gpsimd.indirect_dma_start(
                    out=gath[:, k, :], out_offset=None, in_=table,
                    in_offset=bass.IndirectOffsetOnAxis(ap=gidx[:, k:k + 1], axis=0),
                    bounds_check=last_row, oob_is_err=False).then_inc(s.gathered[k], 16)
            return take_idx, gather

        @block.gpsimd
        def _(pool):
            last_row = pool.to_reg(N - 1)
            pool.wait_ge(setup_done, 1)
            slow = pool.value_load(general_i[0:1, 0:1], min_val=0, max_val=1)

            def general_sums(n, table):
                pool.wait_ge(rows_in_dram, 32)
                zeros = prod[:, :, :].rearrange("p s w -> p (s w)")[:, 0:ZERO_ROWS // P * D]
                nc.gpsimd.memset(zeros, 0.0).then_inc(zero_tile, 1)
                pool.wait_ge(zero_tile, n + 1)
                for a in range(0, N, ZERO_ROWS):
                    a = min(a, N - ZERO_ROWS)
                    pool.dma_start(sums[a:a + ZERO_ROWS, :].rearrange("(p t) d -> p (t d)", p=P), zeros).then_inc(sums_zero, 16)
                    pool.wait_ge(sums_zero, 16 * (n * -(-N // ZERO_ROWS) + -(-(a + ZERO_ROWS) // ZERO_ROWS)))
                with pool.Fori(0, CHUNKS) as c:
                    i = c + n * CHUNKS
                    pool.dma_start(ch_rows[:], edge_rows[bass.ds(c * P, P), :]).then_inc(ch_in, 16)
                    one = bass.AP(dst_flat.tensor, c * P, [[0, P], [1, P]])
                    pool.dma_start(ch_dst[:], one).then_inc(ch_in, 16)
                    pool.wait_ge(ch_in, i * 32 + 32)
                    pool.nop(nofuse=True)
                    nc.gpsimd.tensor_copy(ch_idx[:], ch_rows[:, SOURCE:SOURCE + 1]).then_inc(ch_idx_ready, 1)
                    pool.wait_ge(ch_idx_ready, i + 1)
                    pool.nop(nofuse=True)
                    nc.gpsimd.indirect_dma_start(
                        out=gath[:, 0, :], out_offset=None, in_=table,
                        in_offset=bass.IndirectOffsetOnAxis(ap=ch_idx[:], axis=0),
                        bounds_check=last_row, oob_is_err=False).then_inc(ch_gathered, 16)
                    pool.wait_ge(ch_to_ready, i + 1)
                    pool.nop(nofuse=True)
                    nc.gpsimd.indirect_dma_start(
                        out=ch_old[:], out_offset=None, in_=sums,
                        in_offset=bass.IndirectOffsetOnAxis(ap=ch_to[:], axis=0),
                        bounds_check=last_row, oob_is_err=False).then_inc(ch_before_in, 16)
                    pool.wait_ge(ch_ready, i + 1)
                    pool.nop(nofuse=True)
                    nc.gpsimd.indirect_dma_start(
                        out=sums, out_offset=bass.IndirectOffsetOnAxis(ap=ch_to[:], axis=0), in_=ch_sum[:],
                        in_offset=None, bounds_check=last_row, oob_is_err=False).then_inc(ch_stored, 16)
                    pool.wait_ge(ch_stored, i * 16 + 16)

            for n, table in enumerate((x, hidden, mid)):
                s = passes[n]
                if n:
                    pass_stored(pool, passes[n - 1])
                if n < 2:
                    prime(pool, s.pair)

                def add_pairs(u, k, g, s=s):
                    pool.wait_ge(s.prod, u + 1 + U)
                    pool.wait_ge(s.msg, u - 2 + 1 + U)
                    nc.gpsimd.tensor_tensor(pair[:, k % 2, :], prod[:, k % 2, 0:W4 // 2], prod[:, k % 2, W4 // 2:W4],
                                            ALU.add).then_inc(s.pair, 1)

                def tiles(rows_of, s=s, n=n, add_pairs=add_pairs):
                    take_idx, gather = gathers(pool, s, rows_of, s.prod if n < 2 else s.n_ps, last_row)
                    if n < 2:
                        run_ahead(pool, [(take_idx, 8), (gather, 5), (add_pairs, 0)], T)
                    else:
                        run_ahead(pool, [(take_idx, 20), (gather, 17), (finish, 0)], T)

                if n == 2:
                    prime(pool, s.final)

                def finish(u, k, g, s=s):
                    pool.wait_ge(s.shift, half_count(u, k, g))
                    slot_stored(pool, s, k, g)
                    pool.nop(nofuse=True)
                    nc.gpsimd.tensor_scalar(ht[:, k, :], res[:, k, :], st_rstd[:, k:k + 1], st_shift[:, k:k + 1],
                                            ALU.mult, ALU.add).then_inc(s.final, 1)

                with pool.If(slow):
                    general_sums(n, table)
                    tiles(sums)
                with pool.Else():
                    tiles(table)

        def evacuate(act, s, to, of, done, ready, freed, banks=1):
            def op(u, k, g):
                act.wait_ge(ready, u + 1 + U)
                act.wait_ge(freed, u - 2 + 1 + U)
                nc.scalar.copy(to[:, k % 2, :], of[:, k % banks, :]).then_inc(done, 1)
            return op

        def normalise(act, s, to):
            def squares(u, k, g):
                act.wait_ge(s.neg, half_count(u, k, g))
                act.wait_ge(s.final, u - U + 1 + U)
                act.wait_ge(s.sq, u - 2 + 1 + U)
                nc.scalar.activation(junk[:, k % 2, :], res[:, k, :], ACT.Square, bias=st_neg[:, k:k + 1],
                                     accum_out=st_sq[:, k:k + 1]).then_inc(s.sq, 1)

            def deviation(u, k, g):
                a = half_slots(u, k)
                if a:
                    act.wait_ge(s.sq, u + 1 + U)
                    nc.scalar.activation(st_root[:, a], st_sq[:, a], ACT.Sqrt, bias=eps[:],
                                         scale=1.0 / D).then_inc(s.root, 1)

            def finish(u, k, g):
                act.wait_ge(s.shift, half_count(u, k, g))
                slot_stored(act, s, k, g)
                nc.scalar.activation(to[:, k, :], res[:, k, :], ACT.Identity, bias=st_shift[:, k:k + 1],
                                     scale=st_rstd[:, k:k + 1]).then_inc(s.final, 1)
            return squares, deviation, finish

        @block.scalar
        def _(act):
            for n in (0, 1):
                s = passes[n]
                if n:
                    pass_stored(act, passes[n - 1])
                prime(act, s.xT, s.hotT, s.final, *([s.sq] if n else []))
                to_xT = evacuate(act, s, xT, ps_x, s.xT, s.xT_ps, s.o_ps)
                to_hotT = evacuate(act, s, rel_hotT, ps_r, s.hotT, s.hot_ps, s.w_ps)

                def relu(u, k, g, s=s):
                    act.wait_ge(s.o_ps, u + 1 + U)
                    slot_stored(act, s, k, g)
                    nc.scalar.activation(y[:, k, :], ps_o[:, k % 2, 0:D], ACT.Relu).then_inc(s.final, 1)

                if n == 0:
                    run_ahead(act, [(to_hotT, 2), (to_xT, 1), (relu, 0)], T)
                else:
                    squares, deviation, finish = normalise(act, s, y)
                    run_ahead(act, [(to_hotT, 10), (to_xT, 9), (squares, 5), (deviation, 5), (finish, 0)], T)
            s = passes[2]
            pass_stored(act, passes[1])
            prime(act, s.xT, s.mT, s.slant, s.ysq, s.sq)
            to_xT = evacuate(act, s, xT, ps_x, s.xT, s.xT_ps, s.o_ps)
            to_mT = evacuate(act, s, mT, ps_m, s.mT, s.mT_ps, s.o_ps, 2)

            def slanted(u, k, g):
                act.wait_ge(s.o_ps, u + 1 + U)
                act.wait_ge(s.y, u - 2 + 1 + U)
                nc.scalar.mul(slant[:, k % 2, :], ps_o[:, k % 2, 0:D], SLOPE).then_inc(s.slant, 1)

            def y_squares(u, k, g):
                act.wait_ge(s.y, u + 1 + U)
                act.wait_ge(s.final, u - U + 1 + U)
                act.wait_ge(s.ysq, u - 2 + 1 + U)
                nc.scalar.activation(junk[:, 2 + k % 2, :], y[:, k, :], ACT.Square,
                                     accum_out=st_ysq[:, k:k + 1]).then_inc(s.ysq, 1)

            def norms(u, k, g):
                a = half_slots(u, k)
                if a:
                    act.wait_ge(s.clip, half_count(u, k, g))
                    nc.scalar.activation(st_norm[:, a], st_clip[:, a], ACT.Sqrt).then_inc(s.norm, 1)

            squares, deviation, _ = normalise(act, s, ht)
            run_ahead(act, [(to_xT, 12), (to_mT, 12), (slanted, 11), (y_squares, 10), (norms, 9), (squares, 5), (deviation, 4)], T)

        @block.vector
        def _(dve):
            chain = [0]

            def then(ins):
                chain[0] += 1
                ins.then_inc(dve_done, 1)
                dve.wait_ge(dve_done, chain[0])

            nc.vector.memset(pad_key[:], -1.0)
            nc.vector.memset(pad_dst[:], BIG)
            nc.vector.memset(no_keys[:], -1.0)
            nc.vector.memset(pad_rows[:], 0.0)
            nc.vector.memset(gath[:], 0.0)
            nc.vector.memset(ch_old[:], 0.0)
            nc.vector.memset(ones16[:], 1.0)
            nc.vector.memset(ones32[:], 1.0)
            nc.vector.memset(eps[:], EPS)
            nc.vector.memset(below[:], 0.0)
            nc.vector.memset(rows[:], 0.0)
            then(nc.vector.memset(whole[96:P, :], 0.0))
            nc.vector.memset(pad_rows[:, TARGET:TARGET + 1], BIG).then_inc(keys_out, 1)
            dve.wait_ge(loaded, 16 * 9)
            nc.vector.tensor_copy(eye16[:], eye)
            nc.vector.tensor_copy(rows[:, :, SOURCE], words[:, 0, :])
            nc.vector.tensor_copy(dstf[:], words[:, 1, :])
            nc.vector.tensor_copy(rows[:, :, TARGET], words[:, 1, :])
            nc.vector.tensor_copy(rows[:, :, WEIGHT], weight_in[:])
            then(nc.vector.tensor_copy(rows[:, :, RELATION], words[:, 2, :]))
            nc.vector.scalar_tensor_tensor(keys[:], dstf[:], float(REL), rows[:, :, RELATION], ALU.mult,
                                           ALU.add).then_inc(keys_out, 1)
            dve.sem_inc(below_done, 1)
            with dve.Fori(0, EJ // 2) as i:
                for h in range(2):
                    dve.wait_ge(below_done, i * 2 + h + 1)
                    nc.vector.scalar_tensor_tensor(below[:, 1 - h, :], bounds[0:EP, :], dstf[:, bass.ds(i * 2 + h, 1)],
                                                   below[:, h, :], ALU.is_gt, ALU.add).then_inc(below_done, 1)
            dve.wait_ge(dst_halo_in, 16)
            nc.vector.tensor_tensor(unsorted[:, 0, :], dst_halo[:, 1:EJ + 1], dst_halo[:, 0:EJ], ALU.is_lt)
            then(nc.vector.tensor_tensor(unsorted[:, 1, :], dst_halo[:, RUN:RUN + EJ], dst_halo[:, 0:EJ], ALU.is_equal))
            nc.vector.tensor_reduce(trouble[:], unsorted[:].rearrange("p s j -> p (s j)"), AX_X,
                                    ALU.add).then_inc(trouble_found, 1)
            dve.wait_ge(starts_counted, 1)
            then(nc.vector.tensor_copy(row[:, 0, :], ps_o[0:1, 0, 0:NB]))
            then(nc.vector.tensor_tensor(row[:, 1, 0:NB - 1], row[:, 0, 1:NB], row[:, 0, 0:NB - 1], ALU.subtract))
            then(nc.vector.memset(row[:, 1, LAST:T], 0.0))
            then(nc.vector.tensor_reduce(general[:, 0:1], row[:, 1, 0:NB - 1], AX_X, ALU.max))
            then(nc.vector.tensor_scalar(general[:, 1:2], general[:, 0:1], float(P), None, ALU.is_gt))
            dve.wait_ge(trouble_summed, 1)
            then(nc.vector.tensor_tensor(general[:, 2:3], general[:, 1:2], ps_o[0:1, 1, 0:1], ALU.add))
            then(nc.vector.tensor_scalar(general[:, 3:4], general[:, 2:3], 0.5, None, ALU.is_gt))
            nc.vector.tensor_copy(general_i[:], general[:, 3:4]).then_inc(path_known, 1)
            then(nc.vector.scalar_tensor_tensor(row[:, 1, :], bounds[0:1, :], float(EROWS), row[:, 0, :], ALU.add,
                                                ALU.subtract))
            then(nc.vector.scalar_tensor_tensor(row[:, 2, :], row[:, 1, :], general[:, 3:4], row[:, 0, :], ALU.mult,
                                                ALU.add))
            nc.vector.tensor_copy(start_i[:], row[:, 2, :]).then_inc(starts_ready, 1)
            one = halo[:, 0:EJ]
            near = bass.AP(one.tensor, one.offset, [one.ap[0], [1, SHIFTS], [1, EJ]])
            mine = keys[:].rearrange("p (s j) -> p s j", s=1).to_broadcast([EP, SHIFTS, EJ])
            dve.wait_ge(halo_in, 16)
            then(nc.vector.tensor_tensor(equal[:], near, mine, ALU.is_equal))
            then(nc.vector.tensor_reduce(count[:], equal[:].rearrange("p s j -> p j s"), AX_X, ALU.add))
            dve.wait_ge(path_known, 1)
            slow = dve.value_load(general_i[0:1, 0:1], min_val=0, max_val=1)
            with dve.If(slow):
                nc.vector.memset(count[:], 0.0).then_inc(shifts_counted, 1)
                with dve.Fori(0, STEPS) as i:
                    dve.wait_ge(shifts_in, i * 16 + 16)
                    nc.vector.tensor_tensor(equal[:], near, mine, ALU.is_equal).then_inc(shift_equal, 1)
                    dve.wait_ge(shift_equal, i + 1)
                    nc.vector.tensor_reduce(more[:], equal[:].rearrange("p s j -> p j s"), AX_X,
                                            ALU.add).then_inc(shift_more, 1)
                    dve.wait_ge(shift_more, i + 1)
                    nc.vector.tensor_tensor(count[:], count[:], more[:], ALU.add).then_inc(shifts_counted, 1)
                dve.wait_ge(shifts_counted, STEPS + 1)
            nc.vector.reciprocal(rows[:, :, SHARE], count[:]).then_inc(rows_out, 1)
            dve.wait_ge(split_in, 48)
            then(nc.vector.tensor_copy(parts[:], whole[:]))
            then(nc.vector.tensor_tensor(rest[:], whole[:], parts[:], ALU.subtract))
            nc.vector.tensor_copy(parts[32:64, :], rest[32:64, :])
            then(nc.vector.tensor_copy(parts[64:96, :], rest[64:96, :]))
            then(nc.vector.tensor_tensor(whole[64:96, :], rest[64:96, :], parts[64:96, :], ALU.subtract))
            then(nc.vector.tensor_copy(parts[64:96, :], whole[64:96, :]))
            dve.sem_inc(setup_done, 1)
            dve.sem_inc(window_ready, SLOTS)

            def windows(u, k, g):
                m, col = HALF, u - (HALF - 1)
                if isinstance(u, int) and u == LAST:
                    m, col = 1, T
                elif k % HALF != HALF - 1:
                    return
                first, n = u - m + 1, half_count(u, k, g)
                for slot in range(k - m + 1, k + 1):
                    dve.wait_ge(window_in[slot], (g + 1) * 16)
                nc.vector.tensor_tensor(local[:, at(first, m)], edges[:, at(first, m), TARGET],
                                        bounds[:, at(col, m)], ALU.subtract).then_inc(window_local, 1)
                dve.wait_ge(window_local, n)
                nc.vector.tensor_scalar(far[:, 0:m], local[:, at(first, m)], float(P), BIG, ALU.is_ge,
                                        ALU.mult).then_inc(window_far, 1)
                dve.wait_ge(window_far, n)
                nc.vector.tensor_tensor(node_of[:, at(first, m)], edges[:, at(first, m), SOURCE], far[:, 0:m],
                                        ALU.add).then_inc(window_ready, 1)

            def one_hot(s, field, freed):
                def op(u, k, g):
                    dve.wait_ge(window_ready, half_count(u, k, g) + SLOTS)
                    dve.wait_ge(freed, u - 2 + 1 + U)
                    nc.vector.tensor_scalar(node_hot[:, k % 2, :], iota, local[:, at(u)], edges[:, at(u), field],
                                            ALU.is_equal, ALU.mult).then_inc(s.node_hot, 1)
                return op

            def negate_mean(s):
                def op(u, k, g):
                    a = half_slots(u, k)
                    if a:
                        dve.wait_ge(s.sum, u + 1 + U)
                        nc.vector.tensor_scalar(st_neg[:, a], st_sum[:, a], -1.0 / D, None, ALU.mult).then_inc(s.neg, 1)
                return op

            def shift(s):
                def op(u, k, g):
                    a = half_slots(u, k)
                    if a:
                        dve.wait_ge(s.root, half_count(u, k, g))
                        nc.vector.reciprocal(st_rstd[:, a], st_root[:, a]).then_inc(s.rstd, 1)
                        dve.wait_ge(s.rstd, half_count(u, k, g))
                        nc.vector.tensor_tensor(st_shift[:, a], st_neg[:, a], st_rstd[:, a],
                                                ALU.mult).then_inc(s.shift, 1)
                return op

            def general_sums(n):
                with dve.Fori(0, CHUNKS) as c:
                    i = c + n * CHUNKS
                    dve.wait_ge(ch_in, i * 32 + 32)
                    nc.vector.tensor_scalar(ch_same[:], ch_dst[:], ch_rows[:, TARGET:TARGET + 1], None,
                                            ALU.is_equal).then_inc(ch_equal, 1)
                    dve.wait_ge(ch_equal, i + 1)
                    nc.vector.tensor_tensor(ch_before[:], ch_same[:], earlier, ALU.mult).then_inc(ch_pairs, 1)
                    dve.wait_ge(ch_pairs, i + 1)
                    nc.vector.tensor_reduce(ch_dup[:, 0:1], ch_before[:], AX_X, ALU.add).then_inc(ch_count, 1)
                    dve.wait_ge(ch_count, i + 1)
                    nc.vector.tensor_scalar(ch_dup[:, 1:2], ch_dup[:, 0:1], 0.5, BIG, ALU.is_gt,
                                            ALU.mult).then_inc(ch_dups, 1)
                    dve.wait_ge(ch_dups, i + 1)
                    nc.vector.tensor_tensor(ch_to[:], ch_rows[:, TARGET:TARGET + 1], ch_dup[:, 1:2],
                                            ALU.add).then_inc(ch_to_ready, 1)
                    if n < 2:
                        nc.vector.tensor_scalar(rel_hot[:, 0, :], rel_iota, ch_rows[:, RELATION:RELATION + 1], None,
                                                ALU.is_equal).then_inc(ch_hot, 1)
                        dve.wait_ge(ch_hot_ps, i + 1)
                        nc.vector.tensor_copy(rel_hotT[:, 0, :], ps_r[:, 0, :]).then_inc(ch_hotT, 1)
                        dve.wait_ge(ch_w_ps, i + 1)
                        dve.wait_ge(ch_gathered, i * 16 + 16)
                        nc.vector.tensor_tensor(
                            prod[:, 0, :].rearrange("p (i b o) -> p i b o", i=BI, o=BI),
                            ps_w[:, 0, :].rearrange("p (i b o) -> p i b o", i=BI, o=BI),
                            gath[:, 0, :].rearrange("p (b i z) -> p i b z", i=BI, z=1).to_broadcast([P, BI, D // BI, BI]),
                            ALU.mult).then_inc(ch_prod, 1)
                        dve.wait_ge(ch_prod, i + 1)
                        nc.vector.tensor_tensor(pair[:, 0, :], prod[:, 0, 0:W4 // 2], prod[:, 0, W4 // 2:W4],
                                                ALU.add).then_inc(ch_pair, 1)
                        dve.wait_ge(ch_pair, i + 1)
                        nc.vector.tensor_tensor(msg[:, 1, :], pair[:, 0, 0:D], pair[:, 0, D:2 * D],
                                                ALU.add).then_inc(ch_raw, 1)
                        dve.wait_ge(ch_raw, i + 1)
                    else:
                        dve.wait_ge(ch_gathered, i * 16 + 16)
                    raw, factor = (msg[:, 1, :], SHARE) if n < 2 else (gath[:, 0, :], WEIGHT)
                    nc.vector.tensor_scalar(msg[:, 0, :], raw, ch_rows[:, factor:factor + 1], None,
                                            ALU.mult).then_inc(ch_msg, 1)
                    dve.wait_ge(ch_sum_ps, i + 1)
                    dve.wait_ge(ch_before_in, i * 16 + 16)
                    nc.vector.tensor_tensor(ch_sum[:], ps_o[:, 0, 0:D], ch_old[:], ALU.add).then_inc(ch_ready, 1)
                dve.wait_ge(ch_stored, 16 * (n + 1) * CHUNKS)

            for n in (0, 1):
                s = passes[n]
                if n:
                    pass_stored(dve, passes[n - 1])
                with dve.If(slow):
                    general_sums(n)
                prime(dve, s.hot, s.prod, s.msg, s.node_hot, *([s.sum] if n else []))

                def hot(u, k, g, s=s):
                    dve.wait_ge(window_ready, half_count(u, k, g) + SLOTS)
                    dve.wait_ge(s.hot_ps, u - 2 + 1 + U)
                    nc.vector.tensor_scalar(rel_hot[:, k % 2, :], rel_iota, edges[:, at(u), RELATION], None,
                                            ALU.is_equal).then_inc(s.hot, 1)

                def products(u, k, g, s=s):
                    dve.wait_ge(s.w_ps, u + 1 + U)
                    dve.wait_ge(s.gathered[k], (g + 1) * 16 + s.gathered_before[k])
                    dve.wait_ge(s.pair, u - 2 + 1 + U)
                    shape = [P, BI, D // BI, BI]
                    nc.vector.tensor_tensor(
                        prod[:, k % 2, :].rearrange("p (i b o) -> p i b o", i=BI, o=BI),
                        ps_w[:, k % 2, :].rearrange("p (i b o) -> p i b o", i=BI, o=BI),
                        gath[:, k, :].rearrange("p (b i z) -> p i b z", i=BI, z=1).to_broadcast(shape),
                        ALU.mult).then_inc(s.prod, 1)

                def message(u, k, g, s=s):
                    dve.wait_ge(s.pair, u + 1 + U)
                    dve.wait_ge(s.o_ps, u - 2 + 1 + U)
                    nc.vector.tensor_tensor(msg[:, k % 2, :], pair[:, k % 2, 0:D], pair[:, k % 2, D:2 * D],
                                            ALU.add).then_inc(s.msg, 1)

                node_one_hot = one_hot(s, SHARE, s.o_ps)
                if n == 0:
                    run_ahead(dve, [(windows, 12), (message, 0), (node_one_hot, 1), (products, 2), (hot, 4)], T)
                    continue

                def residual(u, k, g, s=s):
                    dve.wait_ge(s.o_ps, u + 1 + U)
                    dve.wait_ge(s.x_in[k // HALF], (g + 1) * 16)
                    dve.wait_ge(s.final, u - U + 1 + U)
                    nc.vector.scalar_tensor_tensor(res[:, k, :], ps_o[:, k % 2, 0:D], 1.0, xt[:, k, :], ALU.mult, ALU.add,
                                                   accum_out=st_sum[:, k:k + 1]).then_inc(s.sum, 1)

                run_ahead(dve, [(residual, 7), (negate_mean(s), 7), (message, 8), (node_one_hot, 9), (products, 10), (hot, 12),
                                (shift(s), 3)], T)

            s = passes[2]
            pass_stored(dve, passes[1])
            with dve.If(slow):
                general_sums(2)
            prime(dve, s.node_hot, s.msg, s.y, s.sum)

            def interact(u, k, g):
                dve.wait_ge(s.n_ps, u + 1 + U)
                dve.wait_ge(s.x_in[k // HALF], (g + 1) * 16)
                dve.wait_ge(s.mT_ps, u - 2 + 1 + U)
                nc.vector.scalar_tensor_tensor(msg[:, k % 2, :], xt[:, k, :], 1.0, ps_n[:, k % 2, :], ALU.add,
                                               ALU.mult).then_inc(s.msg, 1)

            def leaky(u, k, g):
                dve.wait_ge(s.slant, u + 1 + U)
                dve.wait_ge(s.sum, u - U + 1 + U)
                nc.vector.tensor_tensor(y[:, k, :], ps_o[:, k % 2, 0:D], slant[:, k % 2, :], ALU.max).then_inc(s.y, 1)

            def clip(u, k, g):
                a = half_slots(u, k)
                if a:
                    dve.wait_ge(s.ysq, u + 1 + U)
                    nc.vector.tensor_scalar_max(st_clip[:, a], st_ysq[:, a], MIN_NORM ** 2).then_inc(s.clip, 1)

            def inverse_norm(u, k, g):
                a = half_slots(u, k)
                if a:
                    dve.wait_ge(s.norm, half_count(u, k, g))
                    nc.vector.reciprocal(st_scale[:, a], st_norm[:, a]).then_inc(s.scale, 1)

            def residual(u, k, g):
                dve.wait_ge(s.scale, half_count(u, k, g))
                dve.wait_ge(s.y, u + 1 + U)
                dve.wait_ge(s.final, u - U + 1 + U)
                nc.vector.scalar_tensor_tensor(res[:, k, :], y[:, k, :], st_scale[:, k:k + 1], xt[:, k, :], ALU.mult,
                                               ALU.add, accum_out=st_sum[:, k:k + 1]).then_inc(s.sum, 1)

            run_ahead(dve, [(one_hot(s, WEIGHT, s.n_ps), 14), (interact, 13), (leaky, 11), (clip, 10), (inverse_norm, 9), (residual, 7),
                            (negate_mean(s), 7), (shift(s), 3)], T)

        @block.tensor
        def _(pe):
            pe.wait_ge(below_done, EJ + 1)
            nc.tensor.matmul(ps_o[0:1, 0, 0:NB], ones32[0:EP, :], below[:, EJ % 2, :], start=True,
                             stop=True).then_inc(starts_counted, 1)
            pe.wait_ge(trouble_found, 1)
            nc.tensor.matmul(ps_o[0:1, 1, 0:1], ones32[0:EP, :], trouble[:], start=True,
                             stop=True).then_inc(trouble_summed, 1)
            pe.wait_ge(setup_done, 1)
            slow = pe.value_load(general_i[0:1, 0:1], min_val=0, max_val=1)

            def general_sums(n):
                with pe.Fori(0, CHUNKS) as c:
                    i = c + n * CHUNKS
                    if n < 2:
                        pe.wait_ge(ch_hot, i + 1)
                        nc.tensor.transpose(ps_r[:, 0, :], rel_hot[:, 0, :], eye16[:]).then_inc(ch_hot_ps, 1)
                        pe.wait_ge(ch_hotT, i + 1)
                        for a in range(0, W4, 512):
                            last = nc.tensor.matmul(ps_w[:, 0, a:a + 512], rel_hotT[:, 0, :],
                                                    parts[:, n * W4 + a:n * W4 + a + 512], start=True, stop=True)
                        last.then_inc(ch_w_ps, 1)
                    pe.wait_ge(ch_msg, i + 1)
                    nc.tensor.matmul(ps_o[:, 0, 0:D], ch_same[:], msg[:, 0, :], start=True, stop=True).then_inc(ch_sum_ps, 1)
                pe.wait_ge(ch_stored, 16 * (n + 1) * CHUNKS)

            def transpose_rows(s, to, of, ready, freed, done, banks, slots):
                def op(u, k, g):
                    ready(u, k, g)
                    pe.wait_ge(freed, u - banks + 1 + U)
                    for c in range(K):
                        last = nc.tensor.transpose(to[:, k % banks, c * P:(c + 1) * P], of[:, k % slots, c * P:(c + 1) * P], eye)
                    last.then_inc(done, 1)
                return op

            for n, root in enumerate((root1_sb, root2_sb)):
                s = passes[n]
                if n:
                    pass_stored(pe, passes[n - 1])
                with pe.If(slow):
                    general_sums(n)
                prime(pe, s.xT_ps, s.hot_ps, s.w_ps, s.o_ps)
                arrived = s.h_in if n else s.x_in

                def rows_in(u, k, g, arrived=arrived):
                    pe.wait_ge(arrived[k // HALF], (g + 1) * 16)

                def relation_rows(u, k, g, s=s):
                    pe.wait_ge(s.hot, u + 1 + U)
                    pe.wait_ge(s.hotT, u - 1 + 1 + U)
                    nc.tensor.transpose(ps_r[:, 0, :], rel_hot[:, k % 2, :], eye16[:]).then_inc(s.hot_ps, 1)

                def blocks(u, k, g, s=s, n=n):
                    pe.wait_ge(s.hotT, u + 1 + U)
                    pe.wait_ge(s.prod, u - 2 + 1 + U)
                    for c in range(0, W4, 512):
                        last = nc.tensor.matmul(ps_w[:, k % 2, c:c + 512], rel_hotT[:, k % 2, :],
                                                parts[:, n * W4 + c:n * W4 + c + 512], start=True, stop=True)
                    last.then_inc(s.w_ps, 1)

                def root_product(u, k, g, s=s, n=n, root=root):
                    pe.wait_ge(s.xT, u + 1 + U)
                    pe.wait_ge(s.sum if n else s.final, u - 2 + 1 + U)
                    at_bias = 2 * W4 + n * D
                    nc.tensor.matmul(ps_o[:, k % 2, 0:D], ones16[:], parts[:, at_bias:at_bias + D], start=True, stop=False)
                    for c in range(K):
                        nc.tensor.matmul(ps_o[:, k % 2, 0:D], xT[:, k % 2, c * P:(c + 1) * P], root[:, c, :],
                                         start=False, stop=False)

                def add_messages(u, k, g, s=s):
                    pe.wait_ge(s.msg, u + 1 + U)
                    pe.wait_ge(s.node_hot, u + 1 + U)
                    nc.tensor.matmul(ps_o[:, k % 2, 0:D], node_hot[:, k % 2, :], msg[:, k % 2, :], start=False,
                                     stop=True).then_inc(s.o_ps, 1)

                rows = transpose_rows(s, ps_x, ht if n else xt, rows_in, s.xT, s.xT_ps, 1, U)
                run_ahead(pe, [(relation_rows, 2), (rows, 1), (root_product, 0), (blocks, 2), (add_messages, 0)], T)

            s = passes[2]
            pass_stored(pe, passes[1])
            with pe.If(slow):
                general_sums(2)
            prime(pe, s.xT_ps, s.mT_ps, s.n_ps, s.o_ps)

            def rows_in(u, k, g):
                pe.wait_ge(s.x_in[k // HALF], (g + 1) * 16)

            def message_in(u, k, g):
                pe.wait_ge(s.msg, u + 1 + U)

            def neighbours(u, k, g):
                pe.wait_ge(s.node_hot, u + 1 + U)
                pe.wait_ge(s.gathered[k], (g + 1) * 16 + s.gathered_before[k])
                pe.wait_ge(s.msg, u - 2 + 1 + U)
                nc.tensor.matmul(ps_n[:, k % 2, :], node_hot[:, k % 2, :], gath[:, k, :], start=True,
                                 stop=True).then_inc(s.n_ps, 1)

            def layer(u, k, g):
                pe.wait_ge(s.xT, u + 1 + U)
                pe.wait_ge(s.mT, u + 1 + U)
                pe.wait_ge(s.y, u - 2 + 1 + U)
                at_bias = 2 * W4 + 2 * D
                nc.tensor.matmul(ps_o[:, k % 2, 0:D], ones16[:], parts[:, at_bias:at_bias + D], start=True, stop=False)
                for a, w in ((xT, w1_sb), (mT, w2_sb)):
                    for c in range(K):
                        last = nc.tensor.matmul(ps_o[:, k % 2, 0:D], a[:, k % 2, c * P:(c + 1) * P], w[:, c, :],
                                                start=False, stop=a is mT and c == K - 1)
                last.then_inc(s.o_ps, 1)

            rows = transpose_rows(s, ps_x, xt, rows_in, s.xT, s.xT_ps, 1, U)
            messages = transpose_rows(s, ps_m, msg, message_in, s.mT, s.mT_ps, 2, 2)
            run_ahead(pe, [(neighbours, 2), (rows, 1), (messages, 1), (layer, 0)], T)


def laid_out(inputs):
    import numpy as np

    a = {k: np.ascontiguousarray(v) for k, v in inputs.items()}
    N, D = a["x"].shape
    REL, B, BI, _ = a["L0_gnn_W1"].shape
    own = np.zeros((1, BI, B, BI), np.float32)
    own[0, range(BI), :, range(BI)] = 1.0
    whole = np.zeros((32, 2 * BI * D + 3 * D), np.float32)
    for n, name in enumerate(("L0_gnn_W1", "L0_gnn_W2")):
        rows = np.concatenate([a[name].transpose(0, 2, 1, 3), own])
        whole[:REL + 1, n * BI * D:(n + 1) * BI * D] = rows.reshape(REL + 1, -1)
    for row, col, name in ((0, 0, "L0_gnn_bias1"), (0, 1, "L0_gnn_bias2"), (0, 2, "L1_gnn_b1"), (1, 2, "L1_gnn_b2")):
        at = 2 * BI * D + col * D
        whole[row, at:at + D] = a[name]
    return {
        "x": a["x"], "src": a["src"], "dst": a["dst"], "kind": a["edge_type_16"], "weight": a["edge_weight"],
        "whole": whole, "root1": a["L0_gnn_root1"], "root2": a["L0_gnn_root2"],
        "w1t": np.ascontiguousarray(a["L1_gnn_W1"].T), "w2t": np.ascontiguousarray(a["L1_gnn_W2"].T),
        "consts": constants(N, REL), "own_rows": own_edges(N, REL),
    }


def kernel(**inputs):
    import concourse.bacc as _bacc
    from concourse import mybir as _mybir
    from concourse.bass_utils import run_bass_kernel_spmd as _run

    nc = _bacc.Bacc("TRN2", target_bir_lowering=False, num_devices=1)
    arrays = laid_out(inputs)
    args = [nc.dram_tensor(f"in_{k}", v.shape, _mybir.dt.from_np(v.dtype), kind="ExternalInput").ap()
            for k, v in arrays.items()]
    out = nc.dram_tensor("out", arrays["x"].shape, _mybir.dt.float32, kind="ExternalOutput").ap()
    REL, _, BI, _ = inputs["L0_gnn_W1"].shape
    build(nc, *args, out, REL, BI)
    r = _run(nc, [{f"in_{k}": v for k, v in arrays.items()}], core_ids=[0])
    return r.results[0]["out"]
```

```python
from contextlib import ExitStack

import concourse.bass as bass
from concourse import mybir

P = 128
U = 12
GROUP = 3
WINDOWS = 2
SLOTS = U // GROUP
RUN = 8
FIELDS = 8
SOURCE, TARGET, RELATION, SHARE, WEIGHT = range(5)
SHIFTS = 2 * RUN + 1
BIG = float(1 << 21)
EPS = 1e-5
SLOPE = 0.2
MIN_NORM = 1e-12

F32 = mybir.dt.float32
F32R = mybir.dt.float32r
BF16 = mybir.dt.bfloat16
I32 = mybir.dt.int32
ALU = mybir.AluOpType
ACT = mybir.ActivationFunctionType
AX_X = mybir.AxisListType.X


def constants(N, E, REL):
    import numpy as np

    T = -(-N // P)
    cols = np.arange(P)
    part_rows = np.where((cols < 96) & (cols % 32 <= REL), cols % 32, -1)
    firsts = np.arange(0, T, GROUP) * P
    bounds = [*firsts, *(firsts[:-1] + P), N - P, N]
    own_starts = [E + 2 * P + min(P * t, N - P) for t in range(T)]
    tables = (np.arange(GROUP * P), part_rows, bounds, own_starts)
    rows = [np.tile(np.asarray(a, np.float32), (P, 1)) for a in tables]
    bound_cols = np.full((P * -(-len(bounds) // P),), N, np.float32)
    bound_cols[:len(bounds)] = bounds
    earlier = np.tril(np.ones((P, P), np.float32), -1)
    return np.ascontiguousarray(np.concatenate([np.eye(P, dtype=np.float32), *rows, earlier,
                                                bound_cols.reshape(-1, P).T], 1))


def own_edges(N, REL):
    import numpy as np

    own = np.zeros((N, FIELDS), np.float32)
    own[:, SOURCE] = own[:, TARGET] = np.arange(N)
    own[:, RELATION], own[:, SHARE], own[:, WEIGHT] = REL, 1, 1
    return own


def run_ahead(eng, ops, T):
    most = max(lead for _, lead in ops)
    loops = (T - GROUP - most) // U
    for t in range(-most, 0):
        for op, lead in ops:
            if t + lead >= 0:
                op(t + lead, (t + lead) % U, (t + lead) // U)
    with eng.Fori(0, loops) as g:
        for k in range(U):
            for op, lead in ops:
                op(g * U + (k + lead), (k + lead) % U, g + (k + lead) // U)
    for t in range(loops * U, T):
        for op, lead in ops:
            if t + lead < T:
                op(t + lead, (t + lead) % U, (t + lead) // U)


def build(nc, x, src, dst, kind, weight, split_whole, root1, root2, w1t, w2t, consts, own_rows, out, REL, BI):
    N, D = x.shape
    E = src.shape[0]
    W4 = BI * D
    K = D // P
    T = -(-N // P)
    LAST = T - 1
    OVERLAP = P * T - N
    EP = max(k for k in range(1, P + 1) if E % k == 0)
    EJ = E // EP
    EROWS = E + 2 * P
    NB = 2 * -(-T // GROUP) + 1
    GROUPS = -(-T // GROUP)
    CHUNKS = -(-E // P)
    NBC = -(-NB // P)
    ZERO_ROWS = 2 * W4 // D * P
    STEPS = -(-(2 * E + 1) // SHIFTS)
    KEYS_AT = E + SHIFTS
    assert LAST % GROUP == 0 and N >= P and K == 2 and W4 == 1024 and NBC * P <= 512 and REL < 32

    ctx = ExitStack()
    with ctx:
        def sb(name, shape, dt=F32):
            return ctx.enter_context(nc.sbuf_tensor(name, shape, dt))

        def ps(name, shape, dt=F32):
            return ctx.enter_context(nc.psum_tensor(name, shape, dt))

        def sem(name):
            return ctx.enter_context(nc.semaphore(name))

        hidden = nc.dram_tensor("hidden", [N, D], F32).ap()
        mid = nc.dram_tensor("mid", [N, D], F32).ap()
        edge_rows = nc.dram_tensor("edge_rows", [EROWS + N, FIELDS], F32).ap()
        dst_flat = nc.dram_tensor("dst_flat", [1, EROWS], F32).ap()
        key_flat = nc.dram_tensor("key_flat", [1, E + 2 * KEYS_AT], F32).ap()
        sums = nc.dram_tensor("sums", [N, D], F32).ap()

        const = sb("const", [P, consts.shape[1]])
        eye = const[:, 0:P]
        tail = P + GROUP * P
        iota = const[:, P:tail]
        rel_iota = const[:, tail:tail + P]
        bounds = const[:, tail + P:tail + P + NB]
        own_starts = const[0:1, tail + P + NB:tail + P + NB + T]
        earlier = const[:, tail + P + NB + T:tail + 2 * P + NB + T]
        bound_cols = const[:, tail + 2 * P + NB + T:tail + 2 * P + NB + T + NBC]
        eye16 = sb("eye16", [P, P], BF16)
        ones16 = sb("ones16", [P, P], BF16)
        ones32 = sb("ones32", [P, P])
        root1_sb = sb("root1_sb", [P, K, D])
        root2_sb = sb("root2_sb", [P, K, D])
        w1_sb = sb("w1_sb", [P, K, D])
        w2_sb = sb("w2_sb", [P, K, D])
        parts = sb("parts", [P, 2 * W4 + 3 * D], BF16)
        edges = sb("edges", [P, T, FIELDS])
        local = sb("local", [P, T])
        far = sb("far", [P, GROUP])
        node_of = sb("node_of", [P, T], I32)
        xt = sb("xt", [P, U, D])
        ht = sb("ht", [P, U, D])
        res = sb("res", [P, U, D])
        y = sb("y", [P, U, D])
        gath = sb("gath", [P, U, D])
        gidx = sb("gidx", [P, U], I32)
        glocal = sb("glocal", [P, U])
        xT = sb("xT", [P, 4, D])
        x_hi = sb("x_hi", [P, 4, D], F32R)
        x_lo = sb("x_lo", [P, 4, D], F32R)
        m_hi = sb("m_hi", [P, 2, D], F32R)
        m_lo = sb("m_lo", [P, 2, D], F32R)
        w1_hi = sb("w1_hi", [P, K, D], F32R)
        w2_hi = sb("w2_hi", [P, K, D], F32R)
        w1_lo = sb("w1_lo", [P, K, D], F32R)
        w2_lo = sb("w2_lo", [P, K, D], F32R)
        rel_hot = sb("rel_hot", [P, 4, P], BF16)
        rel_hotT = sb("rel_hotT", [P, 4, P], BF16)
        prod = sb("prod", [P, 2, W4])
        pair = sb("pair", [P, 4, W4 // 2])
        raw = sb("raw", [P, 4, D])
        msg_hi = sb("msg_hi", [P, 4, D], F32R)
        msg_lo = sb("msg_lo", [P, 4, D], F32R)
        node_hot = sb("node_hot", [P, 4, GROUP * P], F32R)
        junk = sb("junk", [P, 4, D])
        slant = sb("slant", [P, 2, D])
        st_sum = sb("st_sum", [P, U])
        st_neg = sb("st_neg", [P, U])
        st_sq = sb("st_sq", [P, U])
        st_root = sb("st_root", [P, U])
        st_ysq = sb("st_ysq", [P, U])
        eps = sb("eps", [P, 1])
        st_rstd = sb("st_rstd", [P, U])
        st_shift = sb("st_shift", [P, U])
        st_norm = sb("st_norm", [P, U])
        st_clip = sb("st_clip", [P, U])
        st_scale = sb("st_scale", [P, U])
        words = sb("words", [EP, 3, EJ], I32)
        weight_in = sb("weight_in", [EP, EJ])
        rows = sb("rows", [EP, EJ, FIELDS])
        keys = sb("keys", [EP, EJ])
        no_keys = sb("no_keys", [EP, EJ])
        dstf = sb("dstf", [EP, EJ])
        halo = sb("halo", [EP, EJ + 2 * RUN])
        dst_halo = sb("dst_halo", [EP, EJ + RUN])
        unsorted = sb("unsorted", [EP, 2, EJ])
        trouble = sb("trouble", [EP, 1])
        row = sb("row", [1, 2, NB])
        general = sb("general", [1, 6])
        general_i = sb("general_i", [1, 1], I32)
        count = sb("count", [EP, EJ])
        more = sb("more", [EP, EJ])
        diag = sb("diag", [EP, EP])
        firsts_below = sb("firsts_below", [P, NBC, EP])
        row_of = sb("row_of", [P, 2, NBC])
        row_i = sb("row_i", [P, NBC], I32)
        row_dst = sb("row_dst", [P, NBC, EJ])
        row_below = sb("row_below", [P, NBC, EJ], BF16)
        position = sb("position", [P, 2, NBC])
        starts = sb("starts", [1, 3, T])
        start_i = sb("start_i", [1, T], I32)
        pad_key = sb("pad_key", [1, RUN])
        pad_dst = sb("pad_dst", [1, 2 * P])
        pad_rows = sb("pad_rows", [P, 2, FIELDS])
        whole = ht[:].rearrange("p u d -> p (u d)")[:, 0:2 * W4 + 3 * D]
        rest = y[:].rearrange("p u d -> p (u d)")[:, 0:2 * W4 + 3 * D]
        equal = res[0:EP].rearrange("p u d -> p (u d)").bitcast(BF16)[:, 0:SHIFTS * EJ]
        equal = equal.rearrange("p (s j) -> p s j", s=SHIFTS)

        ch_rows = sb("ch_rows", [P, FIELDS])
        ch_dst = sb("ch_dst", [P, P])
        ch_same = sb("ch_same", [P, P])
        ch_before = sb("ch_before", [P, P])
        ch_idx = sb("ch_idx", [P, 1], I32)
        ch_to = sb("ch_to", [P, 1], I32)
        ch_dup = sb("ch_dup", [P, 2])
        ch_old = sb("ch_old", [P, D])
        ch_sum = sb("ch_sum", [P, D])

        ps_w = ps("ps_w", [P, 2, W4])
        ps_o = ps("ps_o", [P, 2, 512])
        ps_x = ps("ps_x", [P, 1, D])
        ps_r = ps("ps_r", [P, 1, P], BF16)
        ps_n = ps_w[:, 0, :].rearrange("p (s d) -> p s d", s=2)[:, :, 0:D]
        ps_m = ps_w[:, 1, :].rearrange("p (s d) -> p s d", s=2)[:, :, 0:D]

        loaded = sem("loaded")
        dve_done = sem("dve_done")
        firsts_out, firsts_spread = sem("firsts_out"), sem("firsts_spread")
        rows_found, rows_fetched = sem("rows_found"), sem("rows_fetched")
        positions_found = sem("positions_found")
        starts_counted = sem("starts_counted")
        starts_ready = sem("starts_ready")
        keys_out = sem("keys_out")
        keys_in_dram = sem("keys_in_dram")
        halo_in = sem("halo_in")
        rows_out = sem("rows_out")
        rows_in_dram = sem("rows_in_dram")
        window_in = [sem(f"window_in{k}") for k in range(U)]
        window_local = sem("window_local")
        window_far = sem("window_far")
        window_ready = sem("window_ready")
        setup_done = sem("setup_done")
        dst_in_dram = sem("dst_in_dram")
        dst_halo_in = sem("dst_halo_in")
        trouble_found = sem("trouble_found")
        trouble_summed = sem("trouble_summed")
        path_known = sem("path_known")
        no_keys_out = sem("no_keys_out")
        shifts_in = sem("shifts_in")
        shift_steps = sem("shift_steps")
        shifts_counted = sem("shifts_counted")
        sums_zero, zero_tile = sem("sums_zero"), sem("zero_tile")
        ch_in = sem("ch_in")
        ch_idx_ready = sem("ch_idx_ready")
        ch_gathered = sem("ch_gathered")
        ch_hot, ch_hot_ps, ch_hotT, ch_w_ps = sem("ch_hot"), sem("ch_hot_ps"), sem("ch_hotT"), sem("ch_w_ps")
        ch_sum_steps, ch_msg = sem("ch_sum_steps"), sem("ch_msg")
        ch_dup_steps = sem("ch_dup_steps")
        ch_to_ready = sem("ch_to_ready")
        ch_sum_ps = sem("ch_sum_ps")
        ch_before_in = sem("ch_before_in")
        ch_ready = sem("ch_ready")
        ch_stored = sem("ch_stored")
        split_in = sem("split_in")
        weights_split = sem("weights_split")
        part_rounded, part_left = sem("part_rounded"), sem("part_left")
        far_rows_zero = sem("far_rows_zero")

        x_in = [sem(f"x_in{q}") for q in range(SLOTS)]
        gathered = [sem(f"gathered{k}") for k in range(U)]

        class Signals:

            def __init__(self, n):
                def own(name):
                    return sem(f"p{n}_{name}")

                self.x_in = x_in
                self.stored = [own(f"stored{q}") for q in range(SLOTS)]
                self.n = n
                self.gathered = gathered
                self.idx = own("idx")
                self.xT_ps, self.xT = own("xT_ps"), own("xT")
                self.node_hot, self.hi, self.lo = own("node_hot"), own("hi"), own("lo")
                self.o_ps, self.final = own("o_ps"), own("final")
                if n < 3:
                    self.hot, self.hot_ps, self.hotT = own("hot"), own("hot_ps"), own("hotT")
                    self.w_ps, self.prod, self.pair, self.raw = own("w_ps"), own("prod"), own("pair"), own("raw")
                if n == 2:
                    self.h_in = [own(f"h_in{q}") for q in range(SLOTS)]
                if n > 1:
                    self.sum, self.neg, self.sq = own("sum"), own("neg"), own("sq")
                    self.root, self.rstd, self.shift = own("root"), own("rstd"), own("shift")
                if n == 3:
                    self.x_lo, self.m_lo = own("x_lo"), own("m_lo")
                    self.n_ps, self.inter, self.mT_ps, self.mT = own("n_ps"), own("inter"), own("mT_ps"), own("mT")
                    self.slant, self.y, self.ysq = own("slant"), own("y"), own("ysq")
                    self.clip, self.norm, self.scale = own("clip"), own("norm"), own("scale")

            def x_loaded(self, k, g):
                return (g + 1) * 16 + 16 * (self.n - 1) * len(range(k // GROUP, GROUPS, SLOTS))

        passes = [Signals(1), Signals(2), Signals(3)]

        def pass_stored(eng, s):
            for q in range(SLOTS):
                uses = len(range(q, GROUPS, SLOTS))
                eng.wait_ge(s.stored[q], 16 * (uses + 1))

        def prime(eng, *sems):
            for a in sems:
                eng.sem_inc(a, U)

        def at(u, n=1):
            return slice(u, u + n) if isinstance(u, int) else bass.ds(u, n)

        def group_count(u, k, g):
            return (u // GROUP if isinstance(u, int) else g * SLOTS + k // GROUP) + 1


        class Windows:

            def __init__(self, per):
                self.per = per
                self.slots = SLOTS * per
                self.ring = 4
                self.total = (GROUPS - 1) * per + 1

            def __call__(self, u, k, g):
                if k % GROUP >= self.per:
                    return None, None
                slot = k // GROUP * self.per + k % GROUP
                return (u // GROUP if isinstance(u, int) else g * SLOTS + k // GROUP) * self.per + k % GROUP, slot

            def gathers(self, s, slot, g):
                return (g + 1) * 16 + 16 * (s.n - 1) * len(range(slot, self.total, self.slots))

            def of_tile(self, u, k):
                if self.per == GROUP:
                    return [k % GROUP]
                return [0] if k % GROUP == 0 else range(self.per)

            def columns(self, u, k):
                if isinstance(u, int) and u == LAST:
                    return slice(0, P)
                j = k % GROUP
                return slice(j * P, (j + 1) * P if self.per == GROUP else GROUP * P)

            def freed(self, u, k):
                if self.per == GROUP:
                    return u - self.ring + 1
                return u - k % GROUP - GROUP * (self.ring // self.per - 1)

        def group_slots(u, k):
            if isinstance(u, int) and u == LAST:
                return slice(k, k + 1)
            return slice(k - GROUP + 1, k + 1) if k % GROUP == GROUP - 1 else None

        def tile_rows(u, n):
            if isinstance(u, int) and u == LAST:
                return slice(N - P, N)
            return slice(u * P, (u + n) * P) if isinstance(u, int) else bass.ds(u * P, n * P)

        edge_windows, own_windows = Windows(WINDOWS), Windows(GROUP)

        block = ctx.enter_context(nc.Block())

        @block.sync
        def _(sp):
            for to, of in ((const[:], consts), (words[:, 0, :], src.rearrange("(p j) -> p j", p=EP)),
                           (words[:, 1, :], dst.rearrange("(p j) -> p j", p=EP)),
                           (words[:, 2, :], kind.rearrange("(p j) -> p j", p=EP)),
                           (weight_in[:], weight.rearrange("(p j) -> p j", p=EP)),
                           (root1_sb[:], root1.rearrange("(k p) n -> p k n", k=K)),
                           (root2_sb[:], root2.rearrange("(k p) n -> p k n", k=K)),
                           (w1_sb[:], w1t.rearrange("(k p) n -> p k n", k=K)),
                           (w2_sb[:], w2t.rearrange("(k p) n -> p k n", k=K))):
                sp.dma_start(to, of).then_inc(loaded, 16)
            for r in (0, 32, 64):
                sp.dma_start(whole[r:r + 32, :], split_whole).then_inc(split_in, 16)
            sp.wait_ge(keys_out, 2)
            sp.dma_start(dst_flat[0, 0:E].rearrange("(p j) -> p j", p=EP), dstf[:]).then_inc(dst_in_dram, 16)
            sp.dma_start(dst_flat[:, E:EROWS], pad_dst[:]).then_inc(dst_in_dram, 16)
            sp.dma_start(key_flat[0, KEYS_AT:KEYS_AT + E].rearrange("(p j) -> p j", p=EP),
                         keys[:]).then_inc(keys_in_dram, 16)
            sp.dma_start(key_flat[:, KEYS_AT - RUN:KEYS_AT], pad_key[:]).then_inc(keys_in_dram, 16)
            sp.dma_start(key_flat[:, KEYS_AT + E:KEYS_AT + E + RUN], pad_key[:]).then_inc(keys_in_dram, 16)
            sp.dma_start(edge_rows[E:EROWS, :].rearrange("(p t) f -> p (t f)", p=P),
                         pad_rows[:].rearrange("p t f -> p (t f)")).then_inc(rows_in_dram, 16)
            sp.wait_ge(keys_in_dram, 48)
            wide = bass.AP(key_flat.tensor, KEYS_AT - RUN, [[EJ, EP], [1, EJ + 2 * RUN]])
            sp.dma_start(halo[:], wide).then_inc(halo_in, 16)
            sp.wait_ge(dst_in_dram, 32)
            wide = bass.AP(dst_flat.tensor, 0, [[EJ, EP], [1, EJ + RUN]])
            sp.dma_start(dst_halo[:], wide).then_inc(dst_halo_in, 16)
            sp.wait_ge(path_known, 1)
            slow = sp.value_load(general_i[0:1, 0:1], min_val=0, max_val=1)
            with sp.If(slow):
                sp.dma_start(edge_rows[EROWS:EROWS + N, :], own_rows).then_inc(no_keys_out, 16)
                for first in (SHIFTS - RUN, KEYS_AT + E + RUN):
                    sp.dma_start(key_flat[0, first:first + E].rearrange("(p j) -> p j", p=EP),
                                 no_keys[:]).then_inc(no_keys_out, 16)
                sp.dma_start(key_flat[:, KEYS_AT + 2 * E + RUN:KEYS_AT + 2 * (E + RUN)],
                             pad_key[:]).then_inc(no_keys_out, 16)
                sp.wait_ge(no_keys_out, 64)
                with sp.Fori(0, STEPS) as i:
                    sp.wait_ge(shifts_counted, i + 1)
                    wide = bass.AP(key_flat.tensor, i * SHIFTS + (KEYS_AT - E), [[EJ, EP], [1, EJ + 2 * RUN]])
                    sp.dma_start(halo[:], wide).then_inc(shifts_in, 16)
            sp.wait_ge(rows_out, 1)
            sp.dma_start(edge_rows[0:E, :].rearrange("(p j) f -> p (j f)", p=EP),
                         rows[:].rearrange("p j f -> p (j f)")).then_inc(rows_in_dram, 16)
            sp.wait_ge(starts_ready, 1)
            sp.wait_ge(rows_in_dram, 32)

            def window(wins):
                def op(u, k, g):
                    c, slot = wins(u, k, g)
                    if c is None:
                        return
                    sp.wait_ge(window_ready, group_count(u, k, g))
                    start = sp.value_load(start_i[0:1, at(c)], min_val=0, max_val=EROWS + N - P)
                    sp.dma_start(edges[:, at(c), :].rearrange("p t f -> p (t f)"),
                                 edge_rows[bass.ds(start, P), :]).then_inc(window_in[slot], 16)
                return op

            def load(s, ring, arrived, of, freed):
                def op(u, k, g):
                    if k % GROUP:
                        return
                    m = 1 if isinstance(u, int) and u == LAST else GROUP
                    sp.wait_ge(freed, u + (GROUP - 1) - U + 1 + U)
                    sp.dma_start(ring[:, k:k + m, :],
                                 of[tile_rows(u, m), :].rearrange("(t p) d -> p t d", p=P)).then_inc(arrived[k // GROUP], 16)
                return op

            def store(s, ring, to):
                def op(u, k, g):
                    if isinstance(u, int) and u == LAST:
                        sp.wait_ge(s.final, u + 1 + U)
                        sp.dma_start(to[N - P + OVERLAP:N, :], ring[OVERLAP:P, k, :]).then_inc(s.stored[k // GROUP], 16)
                    elif k % GROUP == GROUP - 1:
                        sp.wait_ge(s.final, u + 1 + U)
                        sp.dma_start(to[tile_rows(u - (GROUP - 1), GROUP), :].rearrange("(t p) d -> p t d", p=P),
                                     ring[:, k - (GROUP - 1):k + 1, :]).then_inc(s.stored[k // GROUP], 16)
                return op

            s = passes[0]
            for q in range(SLOTS):
                sp.sem_inc(s.stored[q], 16)

            def first_pass(wins):
                run_ahead(sp, [(window(wins), 21), (load(s, xt, s.x_in, x, s.xT_ps), 12),
                               (store(s, y, hidden), 0)], T)

            with sp.If(slow):
                first_pass(own_windows)
            with sp.Else():
                first_pass(edge_windows)
            pass_stored(sp, s)
            s = passes[1]
            for q in range(SLOTS):
                sp.sem_inc(s.stored[q], 16)
            run_ahead(sp, [(load(s, ht, s.h_in, hidden, s.xT_ps), 18), (load(s, xt, s.x_in, x, s.sum), 15),
                           (store(s, y, mid), 0)], T)
            pass_stored(sp, s)
            s = passes[2]
            for q in range(SLOTS):
                sp.sem_inc(s.stored[q], 16)
            run_ahead(sp, [(load(s, xt, s.x_in, mid, s.sum), 21), (store(s, ht, out), 0)], T)
            pass_stored(sp, s)

        def slot_stored(eng, s, k, g):
            eng.wait_ge(s.stored[k // GROUP], (g + 1) * 16)

        def gathers(pool, s, table, used, last_row, wins):
            def take_idx(u, k, g):
                m = wins.per
                if isinstance(u, int) and u == LAST:
                    m = 1
                elif k % GROUP != GROUP - 1:
                    return
                first, slot = wins(u - (k % GROUP), k - k % GROUP, g)
                pool.wait_ge(window_ready, group_count(u, k, g) + SLOTS)
                pool.wait_ge(used, first + m - wins.slots + U)
                if s.n == 3:
                    nc.gpsimd.tensor_copy(glocal[:, slot:slot + m], local[:, at(first, m)])
                nc.gpsimd.tensor_copy(gidx[:, slot:slot + m], node_of[:, at(first, m)]).then_inc(s.idx, 1)

            def gather(u, k, g):
                c, slot = wins(u, k, g)
                if c is None:
                    return
                pool.wait_ge(s.idx, group_count(u, k, g))
                pool.wait_ge(used, c - wins.slots + 1 + U)
                pool.nop(nofuse=True)
                nc.gpsimd.indirect_dma_start(
                    out=gath[:, slot, :], out_offset=None, in_=table,
                    in_offset=bass.IndirectOffsetOnAxis(ap=gidx[:, slot:slot + 1], axis=0),
                    bounds_check=last_row, oob_is_err=False).then_inc(s.gathered[slot], 16)
            return take_idx, gather

        def message(eng, engine, s, wins):
            def op(u, k, g):
                c, slot = wins(u, k, g)
                if c is None:
                    return
                h = slot % 4
                eng.wait_ge(s.pair, c + 1 + U)
                eng.wait_ge(s.lo, c - 4 + 1 + U)
                if engine is nc.gpsimd:
                    eng.nop(nofuse=True)
                engine.tensor_tensor(raw[:, h, :], pair[:, h, 0:D], pair[:, h, D:2 * D], ALU.add).then_inc(s.raw, 1)
            return op

        def remainder(dve, s, to, of, hi, done, ready, banks, slots):
            def op(u, k, g):
                dve.wait_ge(ready, u + 1 + U)
                dve.wait_ge(s.o_ps, u - slots + 1 + U)
                nc.vector.tensor_tensor(to[:, k % slots, :], of[:, k % banks, :], hi[:, k % slots, :].bitcast(F32),
                                        ALU.subtract).then_inc(done, 1)
            return op

        def one_hot(eng, s, wins, used):
            def op(u, k, g):
                c, slot = wins(u, k, g)
                if c is None:
                    return
                eng.wait_ge(window_ready, group_count(u, k, g) + SLOTS)
                eng.wait_ge(used, wins.freed(u, k) + U)
                cols = wins.columns(u, k)
                if s.n < 3:
                    nc.vector.tensor_scalar(node_hot[:, slot % wins.ring, cols], iota[:, cols], local[:, at(c)], None,
                                            ALU.is_equal).then_inc(s.node_hot, 1)
                else:
                    eng.wait_ge(s.idx, group_count(u, k, g))
                    eng.nop(nofuse=True)
                    nc.gpsimd.tensor_scalar(node_hot[:, slot % wins.ring, cols], iota[:, cols],
                                            glocal[:, slot:slot + 1], None, ALU.is_equal).then_inc(s.node_hot, 1)
            return op

        @block.gpsimd
        def _(pool):
            last_row, last_list_row = pool.to_reg(N - 1), pool.to_reg(EP - 1)
            pool.wait_ge(dst_in_dram, 32)
            pool.wait_ge(rows_found, 1)
            for b in range(NBC):
                pool.nop(nofuse=True)
                nc.gpsimd.indirect_dma_start(
                    out=row_dst[:, b, :], out_offset=None, in_=dst_flat[0, 0:E].rearrange("(p j) -> p j", j=EJ),
                    in_offset=bass.IndirectOffsetOnAxis(ap=row_i[:, b:b + 1], axis=0),
                    bounds_check=last_list_row, oob_is_err=False).then_inc(rows_fetched, 16)
            pool.wait_ge(loaded, 16 * 9)
            for of, hi in ((w1_sb, w1_hi), (w2_sb, w2_hi)):
                nc.gpsimd.tensor_copy(hi[:], of[:]).then_inc(weights_split, 1)
            pool.wait_ge(weights_split, 2)
            for of, hi, lo in ((w1_sb, w1_hi, w1_lo), (w2_sb, w2_hi, w2_lo)):
                nc.gpsimd.tensor_tensor(lo[:], of[:], hi[:].bitcast(F32), ALU.subtract).then_inc(weights_split, 1)
            pool.wait_ge(setup_done, 1)
            slow = pool.value_load(general_i[0:1, 0:1], min_val=0, max_val=1)

            def general_sums(n, table):
                pool.wait_ge(rows_in_dram, 32)
                zeros = prod[:, :, :].rearrange("p s w -> p (s w)")[:, 0:ZERO_ROWS // P * D]
                nc.gpsimd.memset(zeros, 0.0).then_inc(zero_tile, 1)
                pool.wait_ge(zero_tile, n + 1)
                for a in range(0, N, ZERO_ROWS):
                    a = min(a, N - ZERO_ROWS)
                    pool.dma_start(sums[a:a + ZERO_ROWS, :].rearrange("(p t) d -> p (t d)", p=P),
                                   zeros).then_inc(sums_zero, 16)
                    pool.wait_ge(sums_zero, 16 * (n * -(-N // ZERO_ROWS) + -(-(a + ZERO_ROWS) // ZERO_ROWS)))
                with pool.Fori(0, CHUNKS) as c:
                    i = c + n * CHUNKS
                    pool.dma_start(ch_rows[:], edge_rows[bass.ds(c * P, P), :]).then_inc(ch_in, 16)
                    one = bass.AP(dst_flat.tensor, c * P, [[0, P], [1, P]])
                    pool.dma_start(ch_dst[:], one).then_inc(ch_in, 16)
                    pool.wait_ge(ch_in, i * 32 + 32)
                    pool.nop(nofuse=True)
                    nc.gpsimd.tensor_copy(ch_idx[:], ch_rows[:, SOURCE:SOURCE + 1]).then_inc(ch_idx_ready, 1)
                    pool.wait_ge(ch_idx_ready, i + 1)
                    pool.nop(nofuse=True)
                    nc.gpsimd.indirect_dma_start(
                        out=gath[:, 0, :], out_offset=None, in_=table,
                        in_offset=bass.IndirectOffsetOnAxis(ap=ch_idx[:], axis=0),
                        bounds_check=last_row, oob_is_err=False).then_inc(ch_gathered, 16)
                    pool.wait_ge(ch_to_ready, i + 1)
                    pool.nop(nofuse=True)
                    nc.gpsimd.indirect_dma_start(
                        out=ch_old[:], out_offset=None, in_=sums,
                        in_offset=bass.IndirectOffsetOnAxis(ap=ch_to[:], axis=0),
                        bounds_check=last_row, oob_is_err=False).then_inc(ch_before_in, 16)
                    pool.wait_ge(ch_ready, i + 1)
                    pool.nop(nofuse=True)
                    nc.gpsimd.indirect_dma_start(
                        out=sums, out_offset=bass.IndirectOffsetOnAxis(ap=ch_to[:], axis=0), in_=ch_sum[:],
                        in_offset=None, bounds_check=last_row, oob_is_err=False).then_inc(ch_stored, 16)
                    pool.wait_ge(ch_stored, i * 16 + 16)

            for n, table in enumerate((x, hidden, mid)):
                s = passes[n]
                if n:
                    pass_stored(pool, passes[n - 1])
                if n < 2:
                    prime(pool, s.pair, *([s.raw] if n else []))

                def add_pairs(wins, s=s):
                    def op(u, k, g):
                        c, slot = wins(u, k, g)
                        if c is None:
                            return
                        h, a = slot % 2, slot % 4
                        pool.wait_ge(s.prod, c + 1 + U)
                        pool.wait_ge(s.raw, c - 4 + 1 + U)
                        nc.gpsimd.tensor_tensor(pair[:, a, :], prod[:, h, 0:W4 // 2], prod[:, h, W4 // 2:W4],
                                                ALU.add).then_inc(s.pair, 1)
                    return op

                def tiles(rows_of, wins, s=s, n=n, add_pairs=add_pairs):
                    take_idx, gather = gathers(pool, s, rows_of, s.prod if n < 2 else s.lo, last_row, wins)
                    if n == 0:
                        run_ahead(pool, [(take_idx, 10), (gather, 6), (add_pairs(wins), 0)], T)
                    elif n == 1:
                        run_ahead(pool, [(take_idx, 11), (gather, 7), (add_pairs(wins), 1),
                                         (message(pool, nc.gpsimd, s, wins), 0)], T)
                    else:
                        run_ahead(pool, [(take_idx, 23), (gather, 20), (one_hot(pool, s, wins, s.n_ps), 16),
                                         (finish, 0)], T)

                if n == 2:
                    prime(pool, s.final, s.node_hot)

                def finish(u, k, g, s=s):
                    pool.wait_ge(s.shift, group_count(u, k, g))
                    slot_stored(pool, s, k, g)
                    pool.nop(nofuse=True)
                    nc.gpsimd.tensor_scalar(ht[:, k, :], res[:, k, :], st_rstd[:, k:k + 1], st_shift[:, k:k + 1],
                                            ALU.mult, ALU.add).then_inc(s.final, 1)

                with pool.If(slow):
                    general_sums(n, table)
                    tiles(sums, own_windows)
                with pool.Else():
                    tiles(table, edge_windows)

        def evacuate(act, to, of, done, ready, freed, banks, slots):
            def op(u, k, g):
                act.wait_ge(ready, u + 1 + U)
                act.wait_ge(freed, u - slots + 1 + U)
                nc.scalar.copy(to[:, k % slots, :], of[:, k % banks, :]).then_inc(done, 1)
            return op

        def normalise(act, s, to):
            def squares(u, k, g):
                act.wait_ge(s.neg, group_count(u, k, g))
                act.wait_ge(s.final, u - U + 1 + U)
                act.wait_ge(s.sq, u - 2 + 1 + U)
                nc.scalar.activation(junk[:, k % 2, :], res[:, k, :], ACT.Square, bias=st_neg[:, k:k + 1],
                                     accum_out=st_sq[:, k:k + 1]).then_inc(s.sq, 1)

            def deviation(u, k, g):
                a = group_slots(u, k)
                if a:
                    act.wait_ge(s.sq, u + 1 + U)
                    nc.scalar.activation(st_root[:, a], st_sq[:, a], ACT.Sqrt, bias=eps[:],
                                         scale=1.0 / D).then_inc(s.root, 1)

            def finish(u, k, g):
                act.wait_ge(s.shift, group_count(u, k, g))
                slot_stored(act, s, k, g)
                nc.scalar.activation(to[:, k, :], res[:, k, :], ACT.Identity, bias=st_shift[:, k:k + 1],
                                     scale=st_rstd[:, k:k + 1]).then_inc(s.final, 1)
            return squares, deviation, finish

        @block.scalar
        def _(act):
            act.wait_ge(split_in, 48)
            act.wait_ge(far_rows_zero, 1)
            nc.scalar.copy(parts[:], whole).then_inc(part_rounded, 1)
            act.wait_ge(part_left, 1)
            act.wait_ge(part_rounded, 1)
            nc.scalar.copy(parts[32:64, :], rest[32:64, :])
            nc.scalar.copy(parts[64:96, :], rest[64:96, :]).then_inc(part_rounded, 1)
            act.wait_ge(part_left, 2)
            act.wait_ge(part_rounded, 2)
            nc.scalar.copy(parts[64:96, :], whole[64:96, :]).then_inc(part_rounded, 1)
            act.wait_ge(setup_done, 1)
            slow = act.value_load(general_i[0:1, 0:1], min_val=0, max_val=1)

            def high_part(s, field, wins):
                def op(u, k, g):
                    c, slot = wins(u, k, g)
                    if c is None:
                        return
                    if s.n < 3:
                        act.wait_ge(s.raw, c + 1 + U)
                        of = raw[:, slot % 4, :]
                    else:
                        act.wait_ge(window_ready, group_count(u, k, g) + SLOTS)
                        act.wait_ge(s.gathered[slot], wins.gathers(s, slot, g))
                        of = gath[:, slot, :]
                    act.wait_ge(s.o_ps if s.n < 3 else s.n_ps, wins.freed(u, k) + U)
                    act.wait_ge(s.lo, c - wins.ring + 1 + U)
                    nc.scalar.activation(msg_hi[:, slot % wins.ring, :], of, ACT.Copy,
                                         scale=edges[:, at(c), field]).then_inc(s.hi, 1)
                return op

            def relation_rows(s, wins):
                def op(u, k, g):
                    c, slot = wins(u, k, g)
                    if c is None:
                        return
                    act.wait_ge(s.hot_ps, c + 1 + U)
                    act.wait_ge(s.w_ps, c - 4 + 1 + U)
                    nc.scalar.copy(rel_hotT[:, slot % 4, :], ps_r[:, 0, :]).then_inc(s.hotT, 1)
                return op

            for n in (0, 1):
                s = passes[n]
                if n:
                    pass_stored(act, passes[n - 1])
                prime(act, s.xT, s.hotT, s.hi, s.final, *([s.sq] if n else []))
                to_xT = evacuate(act, xT, ps_x, s.xT, s.xT_ps, s.o_ps, 1, 4)

                def relu(u, k, g, s=s):
                    act.wait_ge(s.o_ps, u + 1 + U)
                    slot_stored(act, s, k, g)
                    nc.scalar.activation(y[:, k, :], ps_o[:, k % 2, 0:D], ACT.Relu).then_inc(s.final, 1)

                def tiles(wins, s=s, n=n, relu=relu, to_xT=to_xT):
                    to_hotT, high = relation_rows(s, wins), high_part(s, SHARE, wins)
                    if n == 0:
                        run_ahead(act, [(to_hotT, 9), (to_xT, 1), (relu, 0), (high, 2)], T)
                    else:
                        squares, deviation, finish = normalise(act, s, y)
                        run_ahead(act, [(to_hotT, 21), (to_xT, 13), (high, 13), (squares, 5), (deviation, 5),
                                        (finish, 0)], T)

                with act.If(slow):
                    tiles(own_windows)
                with act.Else():
                    tiles(edge_windows)
            s = passes[2]
            pass_stored(act, passes[1])
            prime(act, s.xT, s.mT, s.hi, s.slant, s.ysq, s.sq)
            to_xT = evacuate(act, x_hi, ps_x, s.xT, s.xT_ps, s.o_ps, 1, 4)
            to_mT = evacuate(act, m_hi, ps_m, s.mT, s.mT_ps, s.o_ps, 2, 2)

            def slanted(u, k, g):
                act.wait_ge(s.o_ps, u + 1 + U)
                act.wait_ge(s.y, u - 2 + 1 + U)
                nc.scalar.mul(slant[:, k % 2, :], ps_o[:, k % 2, 0:D], SLOPE).then_inc(s.slant, 1)

            def y_squares(u, k, g):
                act.wait_ge(s.y, u + 1 + U)
                act.wait_ge(s.final, u - U + 1 + U)
                act.wait_ge(s.ysq, u - 2 + 1 + U)
                nc.scalar.activation(junk[:, 2 + k % 2, :], y[:, k, :], ACT.Square,
                                     accum_out=st_ysq[:, k:k + 1]).then_inc(s.ysq, 1)

            def norms(u, k, g):
                a = group_slots(u, k)
                if a:
                    act.wait_ge(s.clip, group_count(u, k, g))
                    nc.scalar.activation(st_norm[:, a], st_clip[:, a], ACT.Sqrt).then_inc(s.norm, 1)

            squares, deviation, _ = normalise(act, s, ht)

            def tiles(wins):
                run_ahead(act, [(to_xT, 13), (to_mT, 13), (slanted, 11), (high_part(s, WEIGHT, wins), 18),
                                (y_squares, 10), (norms, 9), (squares, 3), (deviation, 3)], T)

            with act.If(slow):
                tiles(own_windows)
            with act.Else():
                tiles(edge_windows)

        @block.vector
        def _(dve):
            chain = [0]

            def then(ins):
                chain[0] += 1
                ins.then_inc(dve_done, 1)
                dve.wait_ge(dve_done, chain[0])

            nc.vector.memset(pad_key[:], -1.0)
            nc.vector.memset(pad_dst[:], BIG)
            nc.vector.memset(no_keys[:], -1.0)
            nc.vector.memset(pad_rows[:], 0.0)
            nc.vector.memset(gath[:], 0.0)
            nc.vector.memset(ch_old[:], 0.0)
            nc.vector.memset(ones16[:], 1.0)
            nc.vector.memset(ones32[:], 1.0)
            nc.vector.memset(eps[:], EPS)
            nc.vector.memset(whole[96:P, :], 0.0).then_inc(far_rows_zero, 1)
            then(nc.vector.memset(rows[:], 0.0))
            nc.vector.memset(pad_rows[:, :, TARGET:TARGET + 1], BIG).then_inc(keys_out, 1)
            dve.wait_ge(loaded, 16 * 9)
            nc.vector.tensor_copy(eye16[:], eye)
            nc.vector.tensor_copy(rows[:, :, SOURCE], words[:, 0, :])
            nc.vector.tensor_copy(dstf[:], words[:, 1, :])
            nc.vector.tensor_copy(rows[:, :, TARGET], words[:, 1, :])
            nc.vector.tensor_copy(rows[:, :, WEIGHT], weight_in[:])
            then(nc.vector.tensor_copy(rows[:, :, RELATION], words[:, 2, :]))
            nc.vector.scalar_tensor_tensor(keys[:], dstf[:], float(REL), rows[:, :, RELATION], ALU.mult,
                                           ALU.add).then_inc(keys_out, 1)
            nc.vector.tensor_scalar(diag[:], eye[0:EP, 0:EP], dstf[:, 0:1], None, ALU.mult).then_inc(firsts_out, 1)
            dve.wait_ge(firsts_spread, 1)
            shape = [P, NBC, EP]
            then(nc.vector.tensor_tensor(
                firsts_below[:], bound_cols.rearrange("p (b z) -> p b z", z=1).to_broadcast(shape),
                ps_x[:, 0, 0:EP].rearrange("p (z e) -> p z e", z=1).to_broadcast(shape), ALU.is_gt))
            then(nc.vector.tensor_reduce(row_of[:, 0, :], firsts_below[:], AX_X, ALU.add))
            then(nc.vector.tensor_scalar(row_of[:, 1, :], row_of[:, 0, :], -1.0, 0.0, ALU.add, ALU.max))
            nc.vector.tensor_copy(row_i[:], row_of[:, 1, :]).then_inc(rows_found, 1)
            dve.wait_ge(part_rounded, 1)
            nc.vector.tensor_tensor(rest, whole, parts[:], ALU.subtract).then_inc(part_left, 1)
            dve.wait_ge(dst_halo_in, 16)
            nc.vector.tensor_tensor(unsorted[:, 0, :], dst_halo[:, 1:EJ + 1], dst_halo[:, 0:EJ], ALU.is_lt)
            then(nc.vector.tensor_tensor(unsorted[:, 1, :], dst_halo[:, RUN:RUN + EJ], dst_halo[:, 0:EJ], ALU.is_equal))
            nc.vector.tensor_reduce(trouble[:], unsorted[:].rearrange("p s j -> p (s j)"), AX_X,
                                    ALU.add).then_inc(trouble_found, 1)
            dve.wait_ge(rows_fetched, 16 * NBC)
            then(nc.vector.tensor_tensor(
                row_below[:], row_dst[:], bound_cols.rearrange("p (b z) -> p b z", z=1).to_broadcast([P, NBC, EJ]), ALU.is_lt))
            then(nc.vector.tensor_reduce(position[:, 0, :], row_below[:], AX_X, ALU.add))
            nc.vector.scalar_tensor_tensor(position[:, 1, :], row_of[:, 1, :], float(EJ), position[:, 0, :], ALU.mult,
                                           ALU.add).then_inc(positions_found, 1)
            dve.wait_ge(starts_counted, 1)
            then(nc.vector.tensor_copy(row[:, 0, :], ps_o[0:1, 0, 0:NB]))
            G = GROUPS
            nc.vector.tensor_tensor(row[:, 1, 0:G - 1], row[:, 0, 1:G], row[:, 0, 0:G - 1], ALU.subtract)
            nc.vector.tensor_tensor(row[:, 1, G:2 * G - 1], row[:, 0, G:2 * G - 1], row[:, 0, 0:G - 1], ALU.subtract)
            then(nc.vector.tensor_tensor(row[:, 1, 2 * G - 1:2 * G], row[:, 0, 2 * G:NB], row[:, 0, 2 * G - 1:2 * G],
                                         ALU.subtract))
            nc.vector.tensor_reduce(general[:, 0:1], row[:, 1, 0:G - 1], AX_X, ALU.max)
            then(nc.vector.tensor_reduce(general[:, 1:2], row[:, 1, G:2 * G], AX_X, ALU.max))
            then(nc.vector.tensor_scalar(general[:, 2:3], general[:, 0:1], 0.5, None, ALU.mult))
            then(nc.vector.tensor_tensor(general[:, 3:4], general[:, 1:2], general[:, 2:3], ALU.max))
            dve.wait_ge(trouble_summed, 1)
            then(nc.vector.scalar_tensor_tensor(general[:, 4:5], general[:, 3:4], float(P), ps_o[0:1, 1, 0:1], ALU.is_gt,
                                                ALU.add))
            then(nc.vector.tensor_scalar(general[:, 5:6], general[:, 4:5], 0.5, None, ALU.is_gt))
            nc.vector.tensor_copy(general_i[:], general[:, 5:6]).then_inc(path_known, 1)
            then(nc.vector.memset(starts[:, 0, :], 0.0))
            pairs = starts[:, 0, 0:2 * (G - 1)].rearrange("p (g w) -> p g w", w=WINDOWS)
            for w in range(WINDOWS):
                nc.vector.tensor_scalar(pairs[:, :, w], row[:, 0, 0:G - 1], float(w * P), None, ALU.add)
            then(nc.vector.tensor_copy(starts[:, 0, 2 * (G - 1):2 * G - 1], row[:, 0, 2 * G - 1:2 * G]))
            then(nc.vector.tensor_tensor(starts[:, 1, :], own_starts, starts[:, 0, :], ALU.subtract))
            then(nc.vector.scalar_tensor_tensor(starts[:, 2, :], starts[:, 1, :], general[:, 5:6], starts[:, 0, :],
                                                ALU.mult, ALU.add))
            nc.vector.tensor_copy(start_i[:], starts[:, 2, :]).then_inc(starts_ready, 1)
            one = halo[:, 0:EJ]
            near = bass.AP(one.tensor, one.offset, [one.ap[0], [1, SHIFTS], [1, EJ]])
            mine = keys[:].rearrange("p (s j) -> p s j", s=1).to_broadcast([EP, SHIFTS, EJ])
            dve.wait_ge(halo_in, 16)
            then(nc.vector.tensor_tensor(equal, near, mine, ALU.is_equal))
            then(nc.vector.tensor_reduce(count[:], equal.rearrange("p s j -> p j s"), AX_X, ALU.add))
            dve.wait_ge(path_known, 1)
            slow = dve.value_load(general_i[0:1, 0:1], min_val=0, max_val=1)
            with dve.If(slow):
                nc.vector.memset(count[:], 0.0).then_inc(shifts_counted, 1)
                with dve.Fori(0, STEPS) as i:
                    dve.wait_ge(shifts_in, i * 16 + 16)
                    nc.vector.tensor_tensor(equal, near, mine, ALU.is_equal).then_inc(shift_steps, 1)
                    dve.wait_ge(shift_steps, i * 2 + 1)
                    nc.vector.tensor_reduce(more[:], equal.rearrange("p s j -> p j s"), AX_X,
                                            ALU.add).then_inc(shift_steps, 1)
                    dve.wait_ge(shift_steps, i * 2 + 2)
                    nc.vector.tensor_tensor(count[:], count[:], more[:], ALU.add).then_inc(shifts_counted, 1)
                dve.wait_ge(shifts_counted, STEPS + 1)
            nc.vector.reciprocal(rows[:, :, SHARE], count[:]).then_inc(rows_out, 1)
            dve.wait_ge(part_rounded, 2)
            nc.vector.tensor_tensor(whole[64:96, :], rest[64:96, :], parts[64:96, :], ALU.subtract).then_inc(part_left, 1)
            dve.wait_ge(part_rounded, 3)
            dve.sem_inc(setup_done, 1)
            dve.sem_inc(window_ready, SLOTS)

            def windows(wins):
                def op(u, k, g):
                    m, nodes = wins.per, GROUP * P
                    if isinstance(u, int) and u == LAST:
                        m, nodes, col = 1, P, slice(2 * GROUPS - 1, 2 * GROUPS)
                    elif k % GROUP != GROUP - 1:
                        return
                    else:
                        col = at(group_count(u, k, g) - 1)
                    first, slot = wins(u - (k % GROUP), k - k % GROUP, g)
                    n = group_count(u, k, g)
                    for a in range(slot, slot + m):
                        dve.wait_ge(window_in[a], (g + 1) * 16)
                    nc.vector.tensor_scalar(local[:, at(first, m)], edges[:, at(first, m), TARGET],
                                            bounds[:, col], None, ALU.subtract).then_inc(window_local, 1)
                    dve.wait_ge(window_local, n)
                    nc.vector.tensor_scalar(far[:, 0:m], local[:, at(first, m)], float(nodes), BIG, ALU.is_ge,
                                            ALU.mult).then_inc(window_far, 1)
                    dve.wait_ge(window_far, n)
                    nc.vector.tensor_tensor(node_of[:, at(first, m)], edges[:, at(first, m), SOURCE], far[:, 0:m],
                                            ALU.add).then_inc(window_ready, 1)
                return op

            def low_part(s, field, wins, used):
                def op(u, k, g):
                    c, slot = wins(u, k, g)
                    if c is None:
                        return
                    dve.wait_ge(s.hi, c + 1 + U)
                    dve.wait_ge(used, wins.freed(u, k) + U)
                    of = raw[:, slot % 4, :] if s.n < 3 else gath[:, slot, :]
                    nc.vector.scalar_tensor_tensor(msg_lo[:, slot % wins.ring, :], of, edges[:, at(c), field],
                                                   msg_hi[:, slot % wins.ring, :].bitcast(F32), ALU.mult,
                                                   ALU.subtract).then_inc(s.lo, 1)
                return op

            def negate_mean(s):
                def op(u, k, g):
                    a = group_slots(u, k)
                    if a:
                        dve.wait_ge(s.sum, u + 1 + U)
                        nc.vector.tensor_scalar(st_neg[:, a], st_sum[:, a], -1.0 / D, None, ALU.mult).then_inc(s.neg, 1)
                return op

            def shift(s):
                def op(u, k, g):
                    a = group_slots(u, k)
                    if a:
                        dve.wait_ge(s.root, group_count(u, k, g))
                        nc.vector.reciprocal(st_rstd[:, a], st_root[:, a]).then_inc(s.rstd, 1)
                        dve.wait_ge(s.rstd, group_count(u, k, g))
                        nc.vector.tensor_tensor(st_shift[:, a], st_neg[:, a], st_rstd[:, a],
                                                ALU.mult).then_inc(s.shift, 1)
                return op

            def general_sums(n):
                with dve.Fori(0, CHUNKS) as c:
                    i = c + n * CHUNKS
                    dve.wait_ge(ch_in, i * 32 + 32)
                    nc.vector.tensor_scalar(ch_same[:], ch_dst[:], ch_rows[:, TARGET:TARGET + 1], None,
                                            ALU.is_equal).then_inc(ch_dup_steps, 1)
                    dve.wait_ge(ch_dup_steps, i * 4 + 1)
                    nc.vector.tensor_tensor(ch_before[:], ch_same[:], earlier, ALU.mult).then_inc(ch_dup_steps, 1)
                    dve.wait_ge(ch_dup_steps, i * 4 + 2)
                    nc.vector.tensor_reduce(ch_dup[:, 0:1], ch_before[:], AX_X, ALU.add).then_inc(ch_dup_steps, 1)
                    dve.wait_ge(ch_dup_steps, i * 4 + 3)
                    nc.vector.tensor_scalar(ch_dup[:, 1:2], ch_dup[:, 0:1], 0.5, BIG, ALU.is_gt,
                                            ALU.mult).then_inc(ch_dup_steps, 1)
                    dve.wait_ge(ch_dup_steps, i * 4 + 4)
                    nc.vector.tensor_tensor(ch_to[:], ch_rows[:, TARGET:TARGET + 1], ch_dup[:, 1:2],
                                            ALU.add).then_inc(ch_to_ready, 1)
                    if n < 2:
                        nc.vector.tensor_scalar(rel_hot[:, 0, :], rel_iota, ch_rows[:, RELATION:RELATION + 1], None,
                                                ALU.is_equal).then_inc(ch_hot, 1)
                        dve.wait_ge(ch_hot_ps, i + 1)
                        nc.vector.tensor_copy(rel_hotT[:, 0, :], ps_r[:, 0, :]).then_inc(ch_hotT, 1)
                        dve.wait_ge(ch_w_ps, i + 1)
                        dve.wait_ge(ch_gathered, i * 16 + 16)
                        nc.vector.tensor_tensor(
                            prod[:, 0, :].rearrange("p (i b o) -> p i b o", i=BI, o=BI),
                            ps_w[:, 0, :].rearrange("p (i b o) -> p i b o", i=BI, o=BI),
                            gath[:, 0, :].rearrange("p (b i z) -> p i b z", i=BI, z=1).to_broadcast([P, BI, D // BI, BI]),
                            ALU.mult).then_inc(ch_sum_steps, 1)
                        dve.wait_ge(ch_sum_steps, i * 3 + 1)
                        nc.vector.tensor_tensor(pair[:, 0, :], prod[:, 0, 0:W4 // 2], prod[:, 0, W4 // 2:W4],
                                                ALU.add).then_inc(ch_sum_steps, 1)
                        dve.wait_ge(ch_sum_steps, i * 3 + 2)
                        nc.vector.tensor_tensor(raw[:, 1, :], pair[:, 0, 0:D], pair[:, 0, D:2 * D],
                                                ALU.add).then_inc(ch_sum_steps, 1)
                        dve.wait_ge(ch_sum_steps, i * 3 + 3)
                    else:
                        dve.wait_ge(ch_gathered, i * 16 + 16)
                    of, factor = (raw[:, 1, :], SHARE) if n < 2 else (gath[:, 0, :], WEIGHT)
                    nc.vector.tensor_scalar(raw[:, 0, :], of, ch_rows[:, factor:factor + 1], None,
                                            ALU.mult).then_inc(ch_msg, 1)
                    dve.wait_ge(ch_sum_ps, i + 1)
                    dve.wait_ge(ch_before_in, i * 16 + 16)
                    nc.vector.tensor_tensor(ch_sum[:], ps_o[:, 0, 0:D], ch_old[:], ALU.add).then_inc(ch_ready, 1)
                dve.wait_ge(ch_stored, 16 * (n + 1) * CHUNKS)

            for n in (0, 1):
                s = passes[n]
                if n:
                    pass_stored(dve, passes[n - 1])
                with dve.If(slow):
                    general_sums(n)
                prime(dve, s.hot, s.prod, s.node_hot, s.lo, s.sum if n else s.raw)

                def hot(wins, s=s):
                    def op(u, k, g):
                        c, slot = wins(u, k, g)
                        if c is None:
                            return
                        dve.wait_ge(window_ready, group_count(u, k, g) + SLOTS)
                        dve.wait_ge(s.hot_ps, c - 4 + 1 + U)
                        nc.vector.tensor_scalar(rel_hot[:, slot % 4, :], rel_iota, edges[:, at(c), RELATION], None,
                                                ALU.is_equal).then_inc(s.hot, 1)
                    return op

                def products(wins, s=s):
                    def op(u, k, g):
                        c, slot = wins(u, k, g)
                        if c is None:
                            return
                        dve.wait_ge(s.w_ps, c + 1 + U)
                        dve.wait_ge(s.gathered[slot], wins.gathers(s, slot, g))
                        dve.wait_ge(s.pair, c - 2 + 1 + U)
                        shape = [P, BI, D // BI, BI]
                        nc.vector.tensor_tensor(
                            prod[:, slot % 2, :].rearrange("p (i b o) -> p i b o", i=BI, o=BI),
                            ps_w[:, slot % 2, :].rearrange("p (i b o) -> p i b o", i=BI, o=BI),
                            gath[:, slot, :].rearrange("p (b i z) -> p i b z", i=BI, z=1).to_broadcast(shape),
                            ALU.mult).then_inc(s.prod, 1)
                    return op

                def residual(u, k, g, s=s):
                    dve.wait_ge(s.o_ps, u + 1 + U)
                    dve.wait_ge(s.x_in[k // GROUP], s.x_loaded(k, g))
                    dve.wait_ge(s.final, u - U + 1 + U)
                    nc.vector.scalar_tensor_tensor(res[:, k, :], ps_o[:, k % 2, 0:D], 1.0, xt[:, k, :], ALU.mult, ALU.add,
                                                   accum_out=st_sum[:, k:k + 1]).then_inc(s.sum, 1)

                def tiles(wins, s=s, n=n, residual=residual, hot=hot, products=products):
                    node_one_hot, low = one_hot(dve, s, wins, s.o_ps), low_part(s, SHARE, wins, s.o_ps)
                    if n == 0:
                        run_ahead(dve, [(windows(wins), 18), (hot(wins), 12), (low, 1),
                                        (message(dve, nc.vector, s, wins), 3), (node_one_hot, 3),
                                        (products(wins), 7)], T)
                    else:
                        run_ahead(dve, [(low, 12), (residual, 9), (negate_mean(s), 9), (node_one_hot, 12),
                                        (products(wins), 18), (hot(wins), 24), (shift(s), 3)], T)

                with dve.If(slow):
                    tiles(own_windows)
                with dve.Else():
                    tiles(edge_windows)

            s = passes[2]
            pass_stored(dve, passes[1])
            with dve.If(slow):
                general_sums(2)
            prime(dve, s.lo, s.inter, s.y, s.sum, s.x_lo, s.m_lo)
            x_low = remainder(dve, s, x_lo, ps_x, x_hi, s.x_lo, s.xT, 1, 4)
            m_low = remainder(dve, s, m_lo, ps_m, m_hi, s.m_lo, s.mT, 2, 2)

            def interact(u, k, g):
                dve.wait_ge(s.n_ps, u + 1 + U)
                dve.wait_ge(s.x_in[k // GROUP], s.x_loaded(k, g))
                dve.wait_ge(s.mT_ps, u - 4 + 1 + U)
                nc.vector.scalar_tensor_tensor(raw[:, k % 4, :], xt[:, k, :], 1.0, ps_n[:, k % 2, :], ALU.add,
                                               ALU.mult).then_inc(s.inter, 1)

            def leaky(u, k, g):
                dve.wait_ge(s.slant, u + 1 + U)
                dve.wait_ge(s.sum, u - U + 1 + U)
                nc.vector.tensor_tensor(y[:, k, :], ps_o[:, k % 2, 0:D], slant[:, k % 2, :], ALU.max).then_inc(s.y, 1)

            def clip(u, k, g):
                a = group_slots(u, k)
                if a:
                    dve.wait_ge(s.ysq, u + 1 + U)
                    nc.vector.tensor_scalar_max(st_clip[:, a], st_ysq[:, a], MIN_NORM ** 2).then_inc(s.clip, 1)

            def inverse_norm(u, k, g):
                a = group_slots(u, k)
                if a:
                    dve.wait_ge(s.norm, group_count(u, k, g))
                    nc.vector.reciprocal(st_scale[:, a], st_norm[:, a]).then_inc(s.scale, 1)

            def residual(u, k, g):
                dve.wait_ge(s.scale, group_count(u, k, g))
                dve.wait_ge(s.y, u + 1 + U)
                dve.wait_ge(s.final, u - U + 1 + U)
                nc.vector.scalar_tensor_tensor(res[:, k, :], y[:, k, :], st_scale[:, k:k + 1], xt[:, k, :], ALU.mult,
                                               ALU.add, accum_out=st_sum[:, k:k + 1]).then_inc(s.sum, 1)

            def tiles(wins):
                run_ahead(dve, [(interact, 14), (x_low, 13), (m_low, 13), (leaky, 11),
                                (low_part(s, WEIGHT, wins, s.n_ps), 16), (clip, 10), (inverse_norm, 9), (residual, 7),
                                (negate_mean(s), 7), (shift(s), 2)], T)

            with dve.If(slow):
                tiles(own_windows)
            with dve.Else():
                tiles(edge_windows)

        @block.tensor
        def _(pe):
            pe.wait_ge(firsts_out, 1)
            nc.tensor.matmul(ps_x[:, 0, 0:EP], ones32[0:EP, :], diag[:], start=True, stop=True).then_inc(firsts_spread, 1)
            pe.wait_ge(positions_found, 1)
            for b in range(NBC):
                last = nc.tensor.matmul(ps_o[0:1, 0, b * P:(b + 1) * P], position[:, 1, b:b + 1], eye, start=True, stop=True)
            last.then_inc(starts_counted, 1)
            pe.wait_ge(trouble_found, 1)
            nc.tensor.matmul(ps_o[0:1, 1, 0:1], ones32[0:EP, 0:1], trouble[:], start=True,
                             stop=True).then_inc(trouble_summed, 1)
            pe.wait_ge(setup_done, 1)
            slow = pe.value_load(general_i[0:1, 0:1], min_val=0, max_val=1)

            def general_sums(n):
                with pe.Fori(0, CHUNKS) as c:
                    i = c + n * CHUNKS
                    if n < 2:
                        pe.wait_ge(ch_hot, i + 1)
                        nc.tensor.transpose(ps_r[:, 0, :], rel_hot[:, 0, :], eye16[:]).then_inc(ch_hot_ps, 1)
                        pe.wait_ge(ch_hotT, i + 1)
                        for a in range(0, W4, 512):
                            last = nc.tensor.matmul(ps_w[:, 0, a:a + 512], rel_hotT[:, 0, :],
                                                    parts[:, n * W4 + a:n * W4 + a + 512], start=True, stop=True)
                        last.then_inc(ch_w_ps, 1)
                    pe.wait_ge(ch_msg, i + 1)
                    nc.tensor.matmul(ps_o[:, 0, 0:D], ch_same[:], raw[:, 0, :], start=True, stop=True).then_inc(ch_sum_ps, 1)
                pe.wait_ge(ch_stored, 16 * (n + 1) * CHUNKS)

            def add_windows(s, to, wins, u, k, g, start):
                places = wins.of_tile(u, k)
                if isinstance(u, int) and u == LAST:
                    places = [0]
                first, slot = wins(u - (k % GROUP), k - k % GROUP, g)
                pe.wait_ge(s.node_hot, first + places[-1] + 1 + U)
                pe.wait_ge(s.lo, first + places[-1] + 1 + U)
                j = k % GROUP
                for w in places:
                    a = (slot + w) % wins.ring
                    for part in (msg_hi, msg_lo):
                        end = w == places[-1] and part is msg_lo
                        last = nc.tensor.matmul(to, node_hot[:, a, j * P:(j + 1) * P], part[:, a, :],
                                                start=start and w == places[0] and part is msg_hi, stop=end)
                return last

            def transpose_rows(s, to, of, ready, freed, done, banks, slots):
                def op(u, k, g):
                    ready(u, k, g)
                    for a in freed:
                        pe.wait_ge(a, u - banks + 1 + U)
                    for c in range(K):
                        last = nc.tensor.transpose(to[:, k % banks, c * P:(c + 1) * P], of[:, k % slots, c * P:(c + 1) * P], eye)
                    last.then_inc(done, 1)
                return op

            for n, root in enumerate((root1_sb, root2_sb)):
                s = passes[n]
                if n:
                    pass_stored(pe, passes[n - 1])
                with pe.If(slow):
                    general_sums(n)
                prime(pe, s.xT_ps, s.hot_ps, s.w_ps, s.o_ps)

                def rows_in(u, k, g, s=s, n=n):
                    if n:
                        pe.wait_ge(s.h_in[k // GROUP], (g + 1) * 16)
                    else:
                        pe.wait_ge(s.x_in[k // GROUP], s.x_loaded(k, g))

                def relation_rows(wins, s=s):
                    def op(u, k, g):
                        c, slot = wins(u, k, g)
                        if c is None:
                            return
                        pe.wait_ge(s.hot, c + 1 + U)
                        pe.wait_ge(s.hotT, c - 1 + 1 + U)
                        nc.tensor.transpose(ps_r[:, 0, :], rel_hot[:, slot % 4, :], eye16[:]).then_inc(s.hot_ps, 1)
                    return op

                def blocks(wins, s=s, n=n):
                    def op(u, k, g):
                        c, slot = wins(u, k, g)
                        if c is None:
                            return
                        h = slot % 2
                        pe.wait_ge(s.hotT, c + 1 + U)
                        pe.wait_ge(s.prod, c - 2 + 1 + U)
                        for a in range(0, W4, 512):
                            last = nc.tensor.matmul(ps_w[:, h, a:a + 512], rel_hotT[:, slot % 4, :],
                                                    parts[:, n * W4 + a:n * W4 + a + 512], start=True, stop=True)
                        last.then_inc(s.w_ps, 1)
                    return op

                def root_product(u, k, g, s=s, n=n, root=root):
                    pe.wait_ge(s.xT, u + 1 + U)
                    pe.wait_ge(s.sum if n else s.final, u - 2 + 1 + U)
                    at_bias = 2 * W4 + n * D
                    nc.tensor.matmul(ps_o[:, k % 2, 0:D], ones16[:], parts[:, at_bias:at_bias + D], start=True, stop=False)
                    for c in range(K):
                        nc.tensor.matmul(ps_o[:, k % 2, 0:D], xT[:, k % 4, c * P:(c + 1) * P], root[:, c, :],
                                         start=False, stop=False)

                def add_messages(wins, s=s):
                    def op(u, k, g):
                        add_windows(s, ps_o[:, k % 2, 0:D], wins, u, k, g, False).then_inc(s.o_ps, 1)
                    return op

                rows = transpose_rows(s, ps_x, ht if n else xt, rows_in, [s.xT], s.xT_ps, 1, U)

                def tiles(wins, n=n, rows=rows, root_product=root_product, relation_rows=relation_rows, blocks=blocks,
                          add_messages=add_messages):
                    if n == 0:
                        run_ahead(pe, [(blocks(wins), 7), (relation_rows(wins), 9), (rows, 1), (root_product, 0),
                                       (add_messages(wins), 0)], T)
                    else:
                        run_ahead(pe, [(blocks(wins), 8), (relation_rows(wins), 11), (rows, 3), (root_product, 0),
                                       (add_messages(wins), 0)], T)

                with pe.If(slow):
                    tiles(own_windows)
                with pe.Else():
                    tiles(edge_windows)

            s = passes[2]
            pass_stored(pe, passes[1])
            pe.wait_ge(weights_split, 4)
            with pe.If(slow):
                general_sums(2)
            prime(pe, s.xT_ps, s.mT_ps, s.n_ps, s.o_ps)

            def rows_in(u, k, g):
                pe.wait_ge(s.x_in[k // GROUP], s.x_loaded(k, g))

            def message_in(u, k, g):
                pe.wait_ge(s.inter, u + 1 + U)

            def neighbours(wins):
                def op(u, k, g):
                    pe.wait_ge(s.inter, u - 2 + 1 + U)
                    add_windows(s, ps_n[:, k % 2, :], wins, u, k, g, True).then_inc(s.n_ps, 1)
                return op

            def layer(u, k, g):
                pe.wait_ge(s.xT, u + 1 + U)
                pe.wait_ge(s.x_lo, u + 1 + U)
                pe.wait_ge(s.mT, u + 1 + U)
                pe.wait_ge(s.m_lo, u + 1 + U)
                pe.wait_ge(s.y, u - 2 + 1 + U)
                at_bias = 2 * W4 + 2 * D
                nc.tensor.matmul(ps_o[:, k % 2, 0:D], ones16[:], parts[:, at_bias:at_bias + D], start=True, stop=False)
                for hi, lo, w_hi, w_lo, slots in ((x_hi, x_lo, w1_hi, w1_lo, 4), (m_hi, m_lo, w2_hi, w2_lo, 2)):
                    for c in range(K):
                        for a, w in ((hi, w_hi), (lo, w_hi), (hi, w_lo)):
                            end = hi is m_hi and c == K - 1 and w is w_lo
                            last = nc.tensor.matmul(ps_o[:, k % 2, 0:D], a[:, k % slots, c * P:(c + 1) * P], w[:, c, :],
                                                    start=False, stop=end)
                last.then_inc(s.o_ps, 1)

            rows = transpose_rows(s, ps_x, xt, rows_in, [s.xT, s.x_lo], s.xT_ps, 1, U)
            messages = transpose_rows(s, ps_m, raw, message_in, [s.mT, s.m_lo], s.mT_ps, 2, 4)

            def tiles(wins):
                run_ahead(pe, [(neighbours(wins), 2), (rows, 1), (messages, 1), (layer, 0)], T)

            with pe.If(slow):
                tiles(own_windows)
            with pe.Else():
                tiles(edge_windows)


def laid_out(inputs):
    import numpy as np

    a = {k: np.ascontiguousarray(v) for k, v in inputs.items()}
    N, D = a["x"].shape
    REL, B, BI, _ = a["L0_gnn_W1"].shape
    own = np.zeros((1, BI, B, BI), np.float32)
    own[0, range(BI), :, range(BI)] = 1.0
    whole = np.zeros((32, 2 * BI * D + 3 * D), np.float32)
    for n, name in enumerate(("L0_gnn_W1", "L0_gnn_W2")):
        rows = np.concatenate([a[name].transpose(0, 2, 1, 3), own])
        whole[:REL + 1, n * BI * D:(n + 1) * BI * D] = rows.reshape(REL + 1, -1)
    for row, col, name in ((0, 0, "L0_gnn_bias1"), (0, 1, "L0_gnn_bias2"), (0, 2, "L1_gnn_b1"), (1, 2, "L1_gnn_b2")):
        at = 2 * BI * D + col * D
        whole[row, at:at + D] = a[name]
    return {
        "x": a["x"], "src": a["src"], "dst": a["dst"], "kind": a["edge_type_16"], "weight": a["edge_weight"],
        "whole": whole, "root1": a["L0_gnn_root1"], "root2": a["L0_gnn_root2"],
        "w1t": np.ascontiguousarray(a["L1_gnn_W1"].T), "w2t": np.ascontiguousarray(a["L1_gnn_W2"].T),
        "consts": constants(N, a["src"].shape[0], REL), "own_rows": own_edges(N, REL),
    }


def kernel(**inputs):
    import concourse.bacc as _bacc
    from concourse import mybir as _mybir
    from concourse.bass_utils import run_bass_kernel_spmd as _run

    nc = _bacc.Bacc("TRN2", target_bir_lowering=False, num_devices=1)
    arrays = laid_out(inputs)
    args = [nc.dram_tensor(f"in_{k}", v.shape, _mybir.dt.from_np(v.dtype), kind="ExternalInput").ap()
            for k, v in arrays.items()]
    out = nc.dram_tensor("out", arrays["x"].shape, _mybir.dt.float32, kind="ExternalOutput").ap()
    REL, _, BI, _ = inputs["L0_gnn_W1"].shape
    build(nc, *args, out, REL, BI)
    r = _run(nc, [{f"in_{k}": v for k, v in arrays.items()}], core_ids=[0])
    return r.results[0]["out"]
```
